# Optimizing a Trainium2 kernel written in Bass

```python
import numpy as np
import jax
import jax.numpy as jnp

def _softmax(x, axis=-1):
    return jax.nn.softmax(x, axis=axis)

def _gelu(x):
    return jax.nn.gelu(x, approximate=True)

def _silu(x):
    return jax.nn.silu(x)

def _sigmoid(x):
    return jax.nn.sigmoid(x)

def _layernorm(x, axis=-1, eps=1e-05):
    m = jnp.mean(x, axis=axis, keepdims=True)
    v = jnp.var(x, axis=axis, keepdims=True)
    return (x - m) / jnp.sqrt(v + eps)

def _scatter_add(tgt, idx, src, axis=0):
    return tgt.at[idx].add(src)

def _segment_sum(src, seg, n):
    return jax.ops.segment_sum(src, seg, n)
kernel_name = 'mk_cond_resid_d4_seqx_r8_1827f9'

def setup_inputs(seed: int=0):
    np.random.seed(seed)
    _w = jnp.asarray

    def _rec_inputs():
        import jax
        import jax.numpy as jnp
        _rk = jax.random.key(seed)
        x = -7.109e-05 + 0.9999 * jax.random.normal(jax.random.fold_in(_rk, 1), (128, 32, 256), jnp.float32)
        _lenS = 32 - jax.random.randint(jax.random.fold_in(_rk, 7), (128,), 0, max(1, 32 // 4) + 1, jnp.int32)
        _lenS2 = 32 - jax.random.randint(jax.random.fold_in(_rk, 8), (128,), 0, max(1, 32 // 4) + 1, jnp.int32)
        itok_B_1_198 = jax.random.randint(jax.random.fold_in(_rk, 11), (128,), 1, 199, jnp.int32)
        itok_B_0_7 = jax.random.randint(jax.random.fold_in(_rk, 12), (128,), 0, 8, jnp.int32)
        fside_8xS_0 = -0.00162727 + 0.0609077 * jax.random.normal(jax.random.fold_in(_rk, 13), (8, 32), jnp.float32)
        itok_B_0_6 = jax.random.randint(jax.random.fold_in(_rk, 14), (128,), 0, 7, jnp.int32)
        return (x, itok_B_1_198, itok_B_0_7, fside_8xS_0, itok_B_0_6)
    x, itok_B_1_198, itok_B_0_7, fside_8xS_0, itok_B_0_6 = _rec_inputs()

    def _L0_cond_setup():
        import jax, jax.numpy as jnp
        import numpy as np
        B, C, T = (128, 32, 256)
        S, D = (200, 32)
        key = jax.random.key(seed)
        k1, k2, k3 = jax.random.split(key, 3)
        x = jax.random.normal(k1, (B, C, T), dtype=jnp.float32)
        conditions = jax.random.randint(k2, (B,), 0, S, dtype=jnp.int64)
        weights = jax.random.normal(k3, (S, C, D), dtype=jnp.float32) / jnp.sqrt(jnp.float32(C))
        return {'x': x, 'conditions': conditions, 'weights': weights}
    _L0_cond_all = _L0_cond_setup()
    _L0_cond_in = {k: v for k, v in _L0_cond_all.items() if k in ('weights',)}
    del _L0_cond_all

    def _L1_cond_setup():
        import jax, jax.numpy as jnp
        import numpy as np
        B, C, T = (64, 32, 256)
        D, N = (32, 8)
        key = jax.random.key(seed)
        k_x, k_s, k_w, k_b = jax.random.split(key, 4)
        scale = 1.0 / np.sqrt(C)
        x = jax.random.normal(k_x, (B, C, T), dtype=jnp.float32)
        subjects = jax.random.randint(k_s, (B,), 0, N, dtype=jnp.int64)
        weights = jax.random.normal(k_w, (N, C, D), dtype=jnp.float32) * scale
        bias = jax.random.normal(k_b, (N, D), dtype=jnp.float32) * scale
        return {'x': x, 'subjects': subjects, 'weights': weights, 'bias': bias}
    _L1_cond_all = _L1_cond_setup()
    _L1_cond_in = {k: v for k, v in _L1_cond_all.items() if k in ('weights',)}
    del _L1_cond_all

    def _L2_cond_setup():
        import jax, jax.numpy as jnp
        import numpy as np

        def _lora_linear(x, W, A, B, adapter_indices):
            base = jnp.einsum('bsd,df->bsf', x, W)
            Ai = A[adapter_indices]
            Bi = B[adapter_indices]
            lora = jnp.einsum('bsr,brf->bsf', jnp.einsum('bsd,bdr->bsr', x, Ai), Bi)
            return base + lora
        key = jax.random.key(seed)
        ks = jax.random.split(key, 10)
        H, I, N, R = (256, 1024, 8, 16)
        B, S = (4, 256)
        std_h = 1.0 / np.sqrt(H)
        std_i = 1.0 / np.sqrt(I)
        x = jax.random.normal(ks[0], (B, S, H), dtype=jnp.float32)
        adapter_indices = jax.random.randint(ks[1], (B,), 0, N, dtype=jnp.int32)
        Wg = jax.random.normal(ks[2], (H, I), dtype=jnp.float32) * std_h
        Wu = jax.random.normal(ks[3], (H, I), dtype=jnp.float32) * std_h
        Wd = jax.random.normal(ks[4], (I, H), dtype=jnp.float32) * std_i
        Ag = jax.random.normal(ks[5], (N, H, R), dtype=jnp.float32) * std_h
        Bg = jnp.zeros((N, R, I), dtype=jnp.float32) + 0.01
        Au = jax.random.normal(ks[6], (N, H, R), dtype=jnp.float32) * std_h
        Bu = jnp.zeros((N, R, I), dtype=jnp.float32) + 0.01
        Ad = jax.random.normal(ks[7], (N, I, R), dtype=jnp.float32) * std_i
        Bd = jnp.zeros((N, R, H), dtype=jnp.float32) + 0.01
        return {'x': x, 'Wg': Wg, 'Wu': Wu, 'Wd': Wd, 'Ag': Ag, 'Bg': Bg, 'Au': Au, 'Bu': Bu, 'Ad': Ad, 'Bd': Bd, 'adapter_indices': adapter_indices}
    _L2_cond_all = _L2_cond_setup()
    _L2_cond_in = {k: v for k, v in _L2_cond_all.items() if k in ('Wg', 'Wu', 'Wd', 'Ag', 'Bg', 'Au', 'Bu', 'Ad', 'Bd')}
    del _L2_cond_all

    def _L3_cond_setup():
        import jax, jax.numpy as jnp
        import numpy as np
        B, T, D_IN, D_OUT = (16, 256, 256, 256)
        N_ADAPTERS, RANK = (8, 16)
        key = jax.random.key(seed)
        k_x, k_w, k_a, k_b, k_s, k_idx = jax.random.split(key, 6)
        x = jax.random.normal(k_x, (B, T, D_IN), dtype=jnp.float32)
        W = jax.random.normal(k_w, (D_OUT, D_IN), dtype=jnp.float32) * (1.0 / np.sqrt(D_IN))
        A = jax.random.normal(k_a, (N_ADAPTERS, RANK, D_IN), dtype=jnp.float32) * 0.02
        Bm = jax.random.normal(k_b, (N_ADAPTERS, D_OUT, RANK), dtype=jnp.float32) * 0.02
        scalings = jnp.ones((N_ADAPTERS,), dtype=jnp.float32)
        adapter_idx = jax.random.randint(k_idx, (B,), 0, N_ADAPTERS, dtype=jnp.int32)
        return {'x': x, 'W': W, 'A': A, 'Bm': Bm, 'scalings': scalings, 'adapter_idx': adapter_idx}
    _L3_cond_all = _L3_cond_setup()
    _L3_cond_in = {k: v for k, v in _L3_cond_all.items() if k in ('W', 'A', 'Bm', 'scalings')}
    del _L3_cond_all
    return {'x': x, 'itok_B_1_198': itok_B_1_198, 'itok_B_0_7': itok_B_0_7, 'fside_8xS_0': fside_8xS_0, 'itok_B_0_6': itok_B_0_6, 'L0_cond_weights': _L0_cond_in['weights'], 'L1_cond_weights': _L1_cond_in['weights'], 'L2_cond_Wg': _L2_cond_in['Wg'], 'L2_cond_Wu': _L2_cond_in['Wu'], 'L2_cond_Wd': _L2_cond_in['Wd'], 'L2_cond_Ag': _L2_cond_in['Ag'], 'L2_cond_Bg': _L2_cond_in['Bg'], 'L2_cond_Au': _L2_cond_in['Au'], 'L2_cond_Bu': _L2_cond_in['Bu'], 'L2_cond_Ad': _L2_cond_in['Ad'], 'L2_cond_Bd': _L2_cond_in['Bd'], 'L3_cond_W': _L3_cond_in['W'], 'L3_cond_A': _L3_cond_in['A'], 'L3_cond_Bm': _L3_cond_in['Bm'], 'L3_cond_scalings': _L3_cond_in['scalings']}

def reference(x, itok_B_1_198, itok_B_0_7, fside_8xS_0, itok_B_0_6, L0_cond_weights, L1_cond_weights, L2_cond_Wg, L2_cond_Wu, L2_cond_Wd, L2_cond_Ag, L2_cond_Bg, L2_cond_Au, L2_cond_Bu, L2_cond_Ad, L2_cond_Bd, L3_cond_W, L3_cond_A, L3_cond_Bm, L3_cond_scalings):
    import jax
    import jax.numpy as jnp

    def _L0_cond_ref(x, conditions, weights):
        import jax, jax.numpy as jnp
        import numpy as np
        B, C, T = (128, 32, 256)
        S, D = (200, 32)
        w = weights[conditions]
        return jnp.einsum('bct,bcd->bdt', x, w)

    def _L1_cond_ref(x, subjects, weights, bias):
        import jax, jax.numpy as jnp
        import numpy as np
        B, C, T = (64, 32, 256)
        D, N = (32, 8)
        w = weights[subjects]
        b = bias[subjects]
        out = jnp.einsum('bct,bcd->bdt', x, w)
        out = out + b[:, :, None]
        return out

    def _L2_cond_ref(x, Wg, Wu, Wd, Ag, Bg, Au, Bu, Ad, Bd, adapter_indices):
        import jax, jax.numpy as jnp
        import numpy as np

        def _lora_linear(x, W, A, B, adapter_indices):
            base = jnp.einsum('bsd,df->bsf', x, W)
            Ai = A[adapter_indices]
            Bi = B[adapter_indices]
            lora = jnp.einsum('bsr,brf->bsf', jnp.einsum('bsd,bdr->bsr', x, Ai), Bi)
            return base + lora
        gate = _lora_linear(x, Wg, Ag, Bg, adapter_indices)
        up = _lora_linear(x, Wu, Au, Bu, adapter_indices)
        h = jax.nn.silu(gate) * up
        return _lora_linear(h, Wd, Ad, Bd, adapter_indices)

    def _L3_cond_ref(x, W, A, Bm, scalings, adapter_idx):
        import jax, jax.numpy as jnp
        import numpy as np
        B, T, D_IN, D_OUT = (16, 256, 256, 256)
        N_ADAPTERS, RANK = (8, 16)
        H = jnp.einsum('btd,od->bto', x, W)
        A_b = A[adapter_idx]
        B_b = Bm[adapter_idx]
        s_b = scalings[adapter_idx]
        xa = jnp.einsum('btd,brd->btr', x, A_b)
        delta = jnp.einsum('btr,bor->bto', xa, B_b)
        delta = jax.lax.stop_gradient(delta * s_b[:, None, None])
        return H + delta
    x = x + _L0_cond_ref(x, itok_B_1_198, L0_cond_weights)
    x = x + _L1_cond_ref(x, itok_B_0_7, L1_cond_weights, fside_8xS_0)
    x = x + _L2_cond_ref(x, L2_cond_Wg, L2_cond_Wu, L2_cond_Wd, L2_cond_Ag, L2_cond_Bg, L2_cond_Au, L2_cond_Bu, L2_cond_Ad, L2_cond_Bd, itok_B_0_7)
    x = x + _L3_cond_ref(x, L3_cond_W, L3_cond_A, L3_cond_Bm, L3_cond_scalings, itok_B_0_6)
    return x

_drawn_inputs = setup_inputs


def setup_inputs(seed=0):
    import zlib

    import numpy as np

    out = dict(_drawn_inputs(seed))
    spreads = {'L2_cond_Bg': (0.009999999776482582, 0.6),
     'L2_cond_Bu': (0.009999999776482582, 0.6),
     'L2_cond_Bd': (0.009999999776482582, 0.6),
     'L3_cond_scalings': (1.0, 0.6)}
    factors = {'L3_cond_A': 3.021, 'L3_cond_Bm': 2.997}
    for name, (base, spread) in spreads.items():
        noise = np.random.default_rng([zlib.crc32(name.encode()), seed]).standard_normal(out[name].shape)
        drawn = base * np.exp(spread * noise) if base else spread * noise
        out[name] = jnp.asarray(drawn.astype(out[name].dtype))
    for name, factor in factors.items():
        out[name] = (out[name] * factor).astype(out[name].dtype)
    return out
```

```python
from contextlib import ExitStack

import concourse.bass as bass
from concourse import mybir

B, C, T = 128, 32, 256
NSEL, NAD, RANK, FF = 200, 8, 16, 1024
P = 128
NT = B * C
BLK = 512
NBLK = NT // BLK
GRP = BLK // P
BPG = P // C
BPB = BLK // C
KT = T // P
MF = FF // P
WS = 256.0
INV = 1.0 / WS


def build(nc, x, i0, i1, bias, i3, w0, w1, wg, wu, wd, ag, bg, au, bu, ad, bd, w3, a3, bm, scal, out):
    f32, f16, i32, u32 = mybir.dt.float32, mybir.dt.float16, mybir.dt.int32, mybir.dt.uint32
    ALU, ACT = mybir.AluOpType, mybir.ActivationFunctionType

    x_v = x.rearrange("(g b) c t -> (b c) g t", b=BPG)
    out_v = out.rearrange("(g b) c t -> (b c) g t", b=BPG)
    w0_rows = w0.rearrange("s c d -> (s c) d")
    w1_rows = w1.rearrange("s c d -> (s c) d")
    wd_v = wd.rearrange("(p m) n -> p m n", m=MF)
    ad_v = ad.rearrange("n (p m) r -> p n (m r)", m=MF)

    with ExitStack() as ctx:
        def sb(name, shape, dt=f32):
            return ctx.enter_context(nc.sbuf_tensor(name, shape, dt))

        def sem(name):
            return ctx.enter_context(nc.semaphore(name))

        idx = sb("idx", [P, 3, B], i32)
        iota_p = sb("iota_p", [P, 1], i32)
        iota_q = sb("iota_q", [P, 1], i32)
        iota_r = sb("iota_r", [P, P], i32)
        pidx = sb("pidx", [P, 1])
        pmod = sb("pmod", [P, 1])
        ident = sb("ident", [P, P])
        eye32 = sb("eye32", [P, C])
        rows0 = sb("rows0", [P, NT // P], u32)
        rows1 = sb("rows1", [P, NT // P], u32)
        rows0_blk = sb("rows0_blk", [P, GRP], u32)
        rows1_blk = sb("rows1_blk", [P, GRP], u32)
        rel = sb("rel", [P, 2, B])
        ge0 = sb("ge0", [P, 2, B])
        mask2 = sb("mask2", [P, B])
        mask3 = sb("mask3", [P, B])
        mask3s = sb("mask3s", [P, B])
        scol = sb("scol", [P, 1])
        sel1 = sb("sel1", [P, B])
        fraw = sb("fraw", [P, C])
        fhi, fmid, flo, fparts = (sb(n, [P, C], f16) for n in ("fhi", "fmid", "flo", "fparts"))
        fres = sb("fres", [P, C])
        ones = sb("ones", [P, P], f16)

        wgu_raw = sb("wgu_raw", [P, 2, KT, FF])
        wd_raw = sb("wd_raw", [P, MF, T])
        agu_raw = sb("agu_raw", [P, 2, KT, P])
        ad_raw = sb("ad_raw", [P, NAD, MF, RANK])
        ad_f = sb("ad_f", [P, MF, P])
        bgu_raw = sb("bgu_raw", [P, 2, FF])
        bd_raw = sb("bd_raw", [P, T])
        w3_raw = sb("w3_raw", [P, KT, T])
        w3_f = sb("w3_f", [P, KT, T])
        a3_raw = sb("a3_raw", [P, T])
        bm_raw = sb("bm_raw", [P, KT, NAD, RANK])
        ab3_f = sb("ab3_f", [P, 2, T])
        wgu = sb("wgu", [P, 2, 2, KT, MF, P], f16)
        wdd = sb("wdd", [P, 2, MF, T], f16)
        agu = sb("agu", [P, 2, 2, KT, P], f16)
        add = sb("add", [P, 2, MF, P], f16)
        bgu = sb("bgu", [P, 2, 2, MF, P], f16)
        bdd = sb("bdd", [P, 2, T], f16)
        w3t = sb("w3t", [P, 2, KT, T], f16)
        ab3 = sb("ab3", [P, 2, 2, T], f16)

        x0 = sb("x0", [P, GRP, T])
        got0 = sb("got0", [P, GRP, C])
        got1 = sb("got1", [P, GRP, C])
        diag0 = sb("diag0", [P, GRP, P])
        diag1 = sb("diag1", [P, GRP, P])
        x1 = sb("x1", [P, GRP, T])
        bias_rows = sb("bias_rows", [P, BLK], f16)
        x2f = sb("x2f", [P, KT, NT])
        x2s = sb("x2s", [P, 2, KT, BLK], f16)
        zf = sb("zf", [P, 2, BLK])
        zs = sb("zs", [P, 2, 2, BLK], f16)
        silu = sb("silu", [P, 2, BLK])
        hf = sb("hf", [P, 2, BLK])
        hs = sb("hs", [P, 2, MF, BLK], f16)
        zdf = sb("zdf", [P, BLK])
        zds = sb("zds", [P, 2, BLK], f16)
        x3f = sb("x3f", [P, KT, BLK])
        x3s = sb("x3s", [P, 2, KT, BLK], f16)
        z3f = sb("z3f", [P, BLK])
        z3s = sb("z3s", [P, 2, BLK], f16)
        y = sb("y", [P, GRP, T])

        bank = [ctx.enter_context(nc.psum_tensor(f"bank{i}", [P, BLK], f32)) for i in range(8)]
        gate_ps, up_ps = bank[0:2], bank[2:4]
        za_ps, zb_ps = bank[4], bank[5]
        pair_ps = bank[6:8]

        s_idx, s_small, s_x0, s_y = sem("idx_loaded"), sem("small_loaded"), sem("x0_loaded"), sem("y_stored")
        s_w = {k: sem(f"{k}_loaded") for k in ("agu", "wgu0", "wgu1", "bgu", "wd", "ad", "bd", "st3")}
        s_iota, s_rows, s_rowsblk, s_got, s_diag = (sem(n) for n in (
            "iota_done", "rows_done", "rows_blk_done", "rows_gathered", "diag_built"))
        s_zero, s_chain, s_const = sem("zeros_written"), sem("vector_chain"), sem("constants_done")
        s_pre, s_hi, s_lo = sem("weights_scaled"), sem("weights_hi"), sem("weights_lo")
        s_t3, s_t3f = sem("transposed"), sem("transposed_copied")
        s_rb, s_ready = sem("bias_rows_done"), sem("gather_may_start")
        pe_x1, pe_x2, pe_z, pe_gate, pe_up, pe_zd, pe_d, pe_z3, pe_y = (sem(n) for n in (
            "pe_x1", "pe_x2", "pe_z", "pe_gate", "pe_up", "pe_zd", "pe_down", "pe_z3", "pe_y"))
        x1_done, x2f_done, x2hi_done, x2lo_done = sem("x1_done"), sem("x2f_done"), sem("x2hi_done"), sem("x2lo_done")
        zf_done, zhi_done, zlo_done = sem("zf_done"), sem("zhi_done"), sem("zlo_done")
        silu_done, hf_done, hhi_done, hlo_done = sem("silu_done"), sem("hf_done"), sem("hhi_done"), sem("hlo_done")
        zdf_done, zdhi_done, zdlo_done = sem("zdf_done"), sem("zdhi_done"), sem("zdlo_done")
        x3f_done, x3hi_done, x3lo_done = sem("x3f_done"), sem("x3hi_done"), sem("x3lo_done")
        z3f_done, z3hi_done, z3lo_done = sem("z3f_done"), sem("z3hi_done"), sem("z3lo_done")
        y_done = sem("y_done")

        def cols(ap):
            return ap.rearrange("p (c m) -> p m c", m=MF)

        SPLITS = [("agu", agu_raw[:], agu[:, 0], agu[:, 1], WS)]
        for k in range(KT):
            for u in range(2):
                SPLITS.append((f"wgu{k}", cols(wgu_raw[:, u, k, :]), wgu[:, 0, u, k], wgu[:, 1, u, k], WS))
        for u in range(2):
            SPLITS.append(("bgu", cols(bgu_raw[:, u, :]), bgu[:, 0, u], bgu[:, 1, u], WS))
        N_UP = len(SPLITS)
        SPLITS += [("ad", ad_f[:], add[:, 0], add[:, 1], 1.0),
                   ("wd", wd_raw[:], wdd[:, 0], wdd[:, 1], WS),
                   ("bd", bd_raw[:], bdd[:, 0], bdd[:, 1], WS)]
        N_DOWN = len(SPLITS)
        N_ALL = N_DOWN + 2
        W_BYTES = {"agu": 16 * 2 * KT, "wgu0": 32, "wgu1": 32, "bgu": 32, "ad": 16, "wd": 16, "bd": 16}

        def after(eng, s, value):
            if not (isinstance(value, int) and value <= 0):
                eng.wait_ge(s, value)

        block = ctx.enter_context(nc.Block())

        @block.sync
        def _(sp):
            def load_x0(b):
                sp.dma_start(x0[:], x_v[:, bass.ds(b * GRP, GRP), :]).then_inc(s_x0, 16)

            def store(b):
                for h in range(2):
                    sp.wait_ge(y_done, 2 * b + h + 1)
                    sp.dma_start(out_v[:, bass.ds(b * GRP + 2 * h, 2), :], y[:, 2 * h:2 * h + 2, :]).then_inc(s_y, 16)

            for n, v in enumerate((i0, i1, i3)):
                sp.dma_start(idx[:, n, :], v.partition_broadcast(P)).then_inc(s_idx, 16)
            load_x0(0)
            for k in range(KT):
                for u, w in enumerate((wg, wu)):
                    sp.dma_start(wgu_raw[:, u, k, :], w[k * P:(k + 1) * P, :]).then_inc(s_w[f"wgu{k}"], 16)
            sp.dma_start(wd_raw[:], wd_v).then_inc(s_w["wd"], 16)
            sp.wait_ge(pe_x1, 2)
            load_x0(1)
            with sp.Fori(1, NBLK - 1) as j:
                sp.wait_ge(pe_x1, 2 * j + 2)
                load_x0(j + 1)
                store(j - 1)
            store(NBLK - 2)
            store(NBLK - 1)
            sp.wait_ge(s_y, 32 * NBLK)

        @block.gpsimd
        def _(pool):
            nc.gpsimd.memset(fraw[:], 0.0).then_inc(s_zero, 1)
            nc.gpsimd.iota(iota_p[:], pattern=[[0, 1]], base=0, channel_multiplier=1).then_inc(s_iota, 1)
            for q in range(BPG):
                pool.wait_ge(s_iota, q + 1)
                nc.gpsimd.iota(iota_q[q * C:(q + 1) * C, :], pattern=[[0, 1]], base=0,
                               channel_multiplier=1).then_inc(s_iota, 1)
            pool.wait_ge(s_iota, BPG + 1)
            nc.gpsimd.iota(iota_r[:], pattern=[[1, P]], base=0, channel_multiplier=0).then_inc(s_iota, 1)
            nc.gpsimd.memset(diag0[:], 0.0).then_inc(s_zero, 1)
            nc.gpsimd.memset(diag1[:], 0.0).then_inc(s_zero, 1)
            nc.gpsimd.memset(ones[:], INV).then_inc(s_zero, 1)
            pool.wait_ge(s_rows, 2 * BPG)

            def gather(b):
                if not (isinstance(b, int) and b == 0):
                    pool.wait_ge(s_diag, 8 * b)
                    pool.sem_inc(s_ready, 1)
                nc.gpsimd.tensor_copy(rows0_blk[:], rows0[:, bass.ds(b * GRP, GRP)]).then_inc(s_rowsblk, 1)
                nc.gpsimd.tensor_copy(rows1_blk[:], rows1[:, bass.ds(b * GRP, GRP)]).then_inc(s_rowsblk, 1)
                pool.wait_ge(s_rowsblk, 2 * b + 2)
                pool.sem_inc(s_ready, 1)
                for g in range(GRP):
                    for rows, table, got in ((rows0_blk, w0_rows, got0), (rows1_blk, w1_rows, got1)):
                        nc.gpsimd.indirect_dma_start(
                            out=got[:, g, :], out_offset=None, in_=table,
                            in_offset=bass.IndirectOffsetOnAxis(ap=rows[:, g:g + 1], axis=0)).then_inc(s_got, 16)

            gather(0)
            with pool.Fori(1, NBLK) as b:
                gather(b)
            pool.wait_ge(s_got, 16 * 2 * GRP * NBLK)

        @block.tensor
        def _(pe):
            def three(ps, whi, wlo, vhi, vlo, start, stop):
                nc.tensor.matmul(ps, whi, vhi, start=start, stop=False)
                nc.tensor.matmul(ps, wlo, vhi, start=False, stop=False)
                return nc.tensor.matmul(ps, whi, vlo, start=False, stop=stop)

            def mix0(b):
                pe.wait_ge(s_x0, 16 * (b + 1))
                pe.wait_ge(s_diag, 8 * (b + 1))
                for g in range(GRP):
                    last = nc.tensor.matmul(pair_ps[g // 2][:, (g % 2) * T:(g % 2 + 1) * T], diag0[:, g, :],
                                            x0[:, g, :], start=True, stop=True)
                    if g % 2:
                        last.then_inc(pe_x1, 1)

            def mix1(b):
                pe.wait_ge(x1_done, 2 * (b + 1))
                pe.wait_ge(s_rb, b + 1)
                for k in range(KT):
                    nc.tensor.matmul(pair_ps[k][:], ones[:], bias_rows[:], start=True, stop=False)
                    for g in range(GRP):
                        last = nc.tensor.matmul(pair_ps[k][:, g * P:(g + 1) * P], x1[:, g, k * P:(k + 1) * P],
                                                diag1[:, g, :], start=False, stop=g == GRP - 1)
                    last.then_inc(pe_x2, 1)

            def lora3(b):
                pe.wait_ge(x3lo_done, 2 * (b + 1))
                for k in range(KT):
                    cut = slice(k * P, (k + 1) * P)
                    last = three(zb_ps[:], ab3[:, 0, 0, cut], ab3[:, 1, 0, cut], x3s[:, 0, k], x3s[:, 1, k],
                                 k == 0, k == KT - 1)
                last.then_inc(pe_z3, 1)

            def out3(b):
                pe.wait_ge(z3lo_done, b + 1)
                for g in range(GRP):
                    cut = slice(g * P, (g + 1) * P)
                    ps = pair_ps[g // 2][:, (g % 2) * T:(g % 2 + 1) * T]
                    for k in range(KT):
                        three(ps, x3s[:, 0, k, cut], x3s[:, 1, k, cut], w3t[:, 0, k], w3t[:, 1, k], k == 0, False)
                    last = three(ps, z3s[:, 0, cut], z3s[:, 1, cut], ab3[:, 0, 1], ab3[:, 1, 1], False, True)
                    if g % 2:
                        last.then_inc(pe_y, 1)

            def body(j, first, last_block):
                pe.wait_ge(x2lo_done, 2 * (j + 1))
                if first:
                    pe.wait_ge(s_lo, 1)
                else:
                    pe.wait_ge(zdf_done, j)
                for u, ps in enumerate((za_ps, zb_ps)):
                    for k in range(KT):
                        last = three(ps[:], agu[:, 0, u, k], agu[:, 1, u, k], x2s[:, 0, k], x2s[:, 1, k],
                                     k == 0, k == KT - 1)
                    last.then_inc(pe_z, 1)
                if first:
                    pe.wait_ge(s_lo, N_UP)
                for m in range(MF):
                    if not first or m >= 2:
                        pe.wait_ge(silu_done, 8 * j + m - 1)
                        pe.wait_ge(hf_done, 8 * j + m - 1)
                    for u, ps in enumerate((gate_ps[m % 2], up_ps[m % 2])):
                        for k in range(KT):
                            three(ps[:], wgu[:, 0, u, k, m], wgu[:, 1, u, k, m], x2s[:, 0, k], x2s[:, 1, k],
                                  k == 0, False)
                    if m == 0:
                        pe.wait_ge(zlo_done, 2 * (j + 1))
                    for u, (ps, done) in enumerate(((gate_ps[m % 2], pe_gate), (up_ps[m % 2], pe_up))):
                        three(ps[:], bgu[:, 0, u, m], bgu[:, 1, u, m], zs[:, 0, u], zs[:, 1, u],
                              False, True).then_inc(done, 1)
                    if m == 1 and first:
                        pe.wait_ge(s_w["st3"], 16 * 4)
                        for k in range(KT):
                            nc.tensor.transpose(zb_ps[:, k * P:(k + 1) * P], a3_raw[:, k * P:(k + 1) * P], ident[:])
                            last = nc.tensor.transpose(zb_ps[:, T + k * P:T + (k + 1) * P],
                                                       bm_raw[:, k].rearrange("p n r -> p (n r)"), ident[:])
                        last.then_inc(s_t3, 1)
                        for k in range(KT):
                            for o in range(KT):
                                last = nc.tensor.transpose(pair_ps[0][:, k * T + o * P:k * T + (o + 1) * P],
                                                           w3_raw[:, o, k * P:(k + 1) * P], ident[:])
                        last.then_inc(s_t3, 1)
                    if m == 1 and not first:
                        lora3(j - 1)
                    if m == 3 and not first:
                        out3(j - 1)
                    if m == 5 and not last_block:
                        if first:
                            pe.wait_ge(s_t3f, 3)
                        else:
                            pe.wait_ge(y_done, 2 * j)
                        mix0(j + 1)
                if not last_block:
                    mix1(j + 1)
                if first:
                    pe.wait_ge(s_lo, N_DOWN)
                pe.wait_ge(hlo_done, 8 * (j + 1))
                for m in range(MF):
                    last = three(za_ps[:], add[:, 0, m], add[:, 1, m], hs[:, 0, m], hs[:, 1, m], m == 0, m == MF - 1)
                last.then_inc(pe_zd, 1)
                if last_block:
                    pe.wait_ge(y_done, 2 * j)
                else:
                    pe.wait_ge(x2f_done, 2 * (j + 2))
                for c in range(KT):
                    cut = slice(c * P, (c + 1) * P)
                    for m in range(MF):
                        three(pair_ps[c][:], wdd[:, 0, m, cut], wdd[:, 1, m, cut], hs[:, 0, m], hs[:, 1, m],
                              m == 0, False)
                pe.wait_ge(zdlo_done, j + 1)
                for c in range(KT):
                    cut = slice(c * P, (c + 1) * P)
                    three(pair_ps[c][:], bdd[:, 0, cut], bdd[:, 1, cut], zds[:, 0], zds[:, 1],
                          False, True).then_inc(pe_d, 1)

            pe.wait_ge(s_zero, 4)
            mix0(0)
            mix1(0)
            body(0, True, False)
            pe.wait_ge(s_lo, N_ALL)
            with pe.Fori(1, NBLK - 1) as j:
                body(j, False, False)
            body(NBLK - 1, False, True)
            lora3(NBLK - 1)
            out3(NBLK - 1)

        @block.scalar
        def _(act):
            def half(dst, src, scale=1.0):
                return nc.scalar.activation(dst, src, ACT.Copy, scale=scale)

            act.wait_ge(s_zero, 1)
            for q in range(3):
                act.dma_start(fraw[q * C:q * C + NAD, :], bias).then_inc(s_small, 16)
            act.dma_start(scol[:], scal.rearrange("(n a) -> n a", a=1).unsqueeze(1).to_broadcast([NAD, RANK, 1])
                          ).then_inc(s_small, 16)
            for u, a in enumerate((ag, au)):
                for k in range(KT):
                    act.dma_start(agu_raw[:, u, k, :].rearrange("p (n r) -> p n r", n=NAD),
                                  a[:, k * P:(k + 1) * P, :].rearrange("n p r -> p n r")).then_inc(s_w["agu"], 16)
            for u, w in enumerate((bg, bu)):
                act.dma_start(bgu_raw[:, u, :], w.rearrange("n r f -> (n r) f")).then_inc(s_w["bgu"], 16)
            act.dma_start(ad_raw[:].rearrange("p n m r -> p n (m r)"), ad_v).then_inc(s_w["ad"], 16)
            act.dma_start(bd_raw[:], bd.rearrange("n r f -> (n r) f")).then_inc(s_w["bd"], 16)
            act.dma_start(w3_raw[:], w3.rearrange("(o p) i -> p o i", p=P)).then_inc(s_w["st3"], 16)
            act.dma_start(a3_raw[:], a3.rearrange("n r i -> (n r) i")).then_inc(s_w["st3"], 16)
            for k in range(KT):
                act.dma_start(bm_raw[:, k], bm[:, k * P:(k + 1) * P, :].rearrange("n p r -> p n r")
                              ).then_inc(s_w["st3"], 16)

            def x1_copy(b):
                for h in range(2):
                    act.wait_ge(pe_x1, 2 * b + h + 1)
                    half(x1[:, 2 * h:2 * h + 2, :].rearrange("p g t -> p (g t)"), pair_ps[h][:]).then_inc(x1_done, 1)

            def x2_hi(b):
                for k in range(KT):
                    act.wait_ge(x2f_done, 2 * b + k + 1)
                    half(x2s[:, 0, k], x2f[:, k, bass.ds(b * BLK, BLK)]
                         ).then_inc(x2hi_done, 1)

            def y_copy(b):
                for h in range(2):
                    act.wait_ge(pe_y, 2 * b + h + 1)
                    half(y[:, 2 * h:2 * h + 2, :].rearrange("p g t -> p (g t)"), pair_ps[h][:], INV
                         ).then_inc(y_done, 1)

            def z3_hi(b):
                act.wait_ge(z3f_done, b + 1)
                half(z3s[:, 0], z3f[:]).then_inc(z3hi_done, 1)

            def weights_hi(a, b):
                for name, src, hi, _, scale in SPLITS[a:b]:
                    act.wait_ge(s_w[name], W_BYTES[name])
                    if name == "ad":
                        half(ad_f[:].rearrange("p m (n r) -> p m n r", n=NAD),
                             ad_raw[:].rearrange("p n m r -> p m n r"), WS).then_inc(s_pre, 1)
                        act.wait_ge(s_pre, 1)
                    half(hi, src, scale).then_inc(s_hi, 1)

            def h_hi(j, m):
                act.wait_ge(hf_done, 8 * j + m + 1)
                half(hs[:, 0, m], hf[:, m % 2]).then_inc(hhi_done, 1)

            def body(j, first, last_block):
                for u in range(2):
                    act.wait_ge(zf_done, 2 * j + u + 1)
                    half(zs[:, 0, u], zf[:, u]).then_inc(zhi_done, 1)
                if first:
                    weights_hi(N_UP, N_DOWN)
                for m in range(MF):
                    act.wait_ge(pe_gate, 8 * j + m + 1)
                    nc.scalar.activation(silu[:, m % 2], gate_ps[m % 2][:], ACT.Silu, scale=INV
                                         ).then_inc(silu_done, 1)
                    if m:
                        h_hi(j, m - 1)
                    if m == 2 and not first:
                        z3_hi(j - 1)
                    if m == 2 and first:
                        act.wait_ge(s_t3f, 1)
                        half(ab3[:, 0], ab3_f[:], WS).then_inc(s_hi, 1)
                        act.wait_ge(s_t3f, 3)
                        half(w3t[:, 0], w3_f[:], WS).then_inc(s_hi, 1)
                    if m == 4 and not first:
                        y_copy(j - 1)
                    if m == 6 and not last_block:
                        x1_copy(j + 1)
                h_hi(j, MF - 1)
                if not last_block:
                    x2_hi(j + 1)
                act.wait_ge(zdf_done, j + 1)
                half(zds[:, 0], zdf[:]).then_inc(zdhi_done, 1)
                for c in range(KT):
                    act.wait_ge(x3f_done, 2 * j + c + 1)
                    half(x3s[:, 0, c], x3f[:, c]).then_inc(x3hi_done, 1)
                if not first:
                    act.wait_ge(s_y, 32 * j)

            x1_copy(0)
            weights_hi(0, 1)
            x2_hi(0)
            weights_hi(1, N_UP)
            body(0, True, False)
            with act.Fori(1, NBLK - 1) as j:
                body(j, False, False)
            body(NBLK - 1, False, True)
            z3_hi(NBLK - 1)
            y_copy(NBLK - 1)

        @block.vector
        def _(dve):
            chain = [0]

            def link(ins):
                chain[0] += 1
                ins.then_inc(s_chain, 1)
                dve.wait_ge(s_chain, chain[0])

            def lo(dst, src, hi, scale=1.0):
                if scale == 1.0:
                    return nc.vector.tensor_tensor(dst, src, hi, ALU.subtract)
                return nc.vector.scalar_tensor_tensor(dst, src, scale, hi, ALU.mult, ALU.subtract)

            def by_batch(ap, b):
                return ap[:, bass.ds(b * BPB, BPB)].unsqueeze(2).to_broadcast([P, BPB, C])

            def tokens(ap):
                return ap.rearrange("p (b c) -> p b c", c=C)

            def bias_matrix(b):
                nc.vector.tensor_tensor(tokens(bias_rows[:]), fparts[:].unsqueeze(1).to_broadcast([P, BPB, C]),
                                        by_batch(sel1, b), ALU.mult).then_inc(s_rb, 1)

            def diagonals(b):
                dve.wait_ge(s_got, 16 * 2 * GRP * (b + 1))
                for got, diag in ((got0, diag0), (got1, diag1)):
                    for q in range(BPG):
                        rows = slice(q * C, (q + 1) * C)
                        nc.vector.tensor_tensor(
                            diag[rows, :, rows], got[rows, :, :],
                            eye32[rows, :].unsqueeze(1).to_broadcast([C, GRP, C]), ALU.add).then_inc(s_diag, 1)

            def x2_copy(b):
                for k in range(KT):
                    dve.wait_ge(pe_x2, 2 * b + k + 1)
                    dst = x2f[:, k, bass.ds(b * BLK, BLK)]
                    nc.vector.tensor_copy(dst, pair_ps[k][:]).then_inc(x2f_done, 1)

            def x2_lo(b):
                for k in range(KT):
                    dve.wait_ge(x2hi_done, 2 * b + k + 1)
                    src = x2f[:, k, bass.ds(b * BLK, BLK)]
                    lo(x2s[:, 1, k], src, x2s[:, 0, k]).then_inc(x2lo_done, 1)

            def z3_mask(b):
                dve.wait_ge(pe_z3, b + 1)
                nc.vector.tensor_tensor(tokens(z3f[:]), tokens(zb_ps[:]), by_batch(mask3s, b), ALU.mult
                                        ).then_inc(z3f_done, 1)
                dve.wait_ge(z3hi_done, b + 1)
                lo(z3s[:, 1], z3f[:], z3s[:, 0]).then_inc(z3lo_done, 1)
                dve.wait_ge(z3lo_done, b + 1)

            def weights_lo(a, b):
                for n, (_, src, hi, low, scale) in enumerate(SPLITS[a:b], a):
                    dve.wait_ge(s_hi, n + 1)
                    lo(low, src, hi, scale).then_inc(s_lo, 1)

            def h_lo(j, m):
                dve.wait_ge(hhi_done, 8 * j + m + 1)
                lo(hs[:, 1, m], hf[:, m % 2], hs[:, 0, m]).then_inc(hlo_done, 1)

            def body(j, first, last_block):
                for u, ps in enumerate((za_ps, zb_ps)):
                    dve.wait_ge(pe_z, 2 * j + u + 1)
                    after(dve, zlo_done, 2 * j)
                    nc.vector.tensor_tensor(tokens(zf[:, u]), tokens(ps[:]), by_batch(mask2, j), ALU.mult
                                            ).then_inc(zf_done, 1)
                for u in range(2):
                    dve.wait_ge(zhi_done, 2 * j + u + 1)
                    lo(zs[:, 1, u], zf[:, u], zs[:, 0, u]).then_inc(zlo_done, 1)
                if first:
                    weights_lo(N_UP, N_DOWN)
                for m in range(MF):
                    dve.wait_ge(silu_done, 8 * j + m + 1)
                    dve.wait_ge(pe_up, 8 * j + m + 1)
                    if not first or m >= 2:
                        dve.wait_ge(hlo_done, 8 * j + m - 1)
                    nc.vector.scalar_tensor_tensor(hf[:, m % 2], up_ps[m % 2][:], INV, silu[:, m % 2],
                                                   ALU.mult, ALU.mult).then_inc(hf_done, 1)
                    if m:
                        h_lo(j, m - 1)
                    if m == 3 and not last_block:
                        bias_matrix(j + 1)
                        diagonals(j + 1)
                    if m == 2 and not first:
                        z3_mask(j - 1)
                    if m == 2 and first:
                        dve.wait_ge(s_t3, 1)
                        nc.vector.tensor_copy(ab3_f[:].rearrange("p a t -> p (a t)"), zb_ps[:]).then_inc(s_t3f, 1)
                        dve.wait_ge(s_t3, 2)
                        for k in range(KT):
                            other = slice((1 - k) * P, (2 - k) * P)
                            link(nc.vector.tensor_copy(w3_f[:, k, other], pair_ps[0][:, k * T + (1 - k) * P:
                                                                                     k * T + (2 - k) * P]))
                            nc.vector.tensor_tensor(w3_f[:, k, k * P:(k + 1) * P],
                                                    pair_ps[0][:, k * T + k * P:k * T + (k + 1) * P],
                                                    ident[:], ALU.add).then_inc(s_t3f, 1)
                        dve.wait_ge(s_hi, N_DOWN + 1)
                        lo(ab3[:, 1], ab3_f[:], ab3[:, 0], WS).then_inc(s_lo, 1)
                        dve.wait_ge(s_hi, N_DOWN + 2)
                        lo(w3t[:, 1], w3_f[:], w3t[:, 0], WS).then_inc(s_lo, 1)
                h_lo(j, MF - 1)
                if not last_block:
                    x2_copy(j + 1)
                    x2_lo(j + 1)
                dve.wait_ge(pe_zd, j + 1)
                after(dve, zdlo_done, j)
                nc.vector.tensor_tensor(tokens(zdf[:]), tokens(za_ps[:]), by_batch(mask2, j), ALU.mult
                                        ).then_inc(zdf_done, 1)
                dve.wait_ge(zdhi_done, j + 1)
                lo(zds[:, 1], zdf[:], zds[:, 0]).then_inc(zdlo_done, 1)
                for c in range(KT):
                    dve.wait_ge(pe_d, 2 * j + c + 1)
                    after(dve, x3lo_done, 2 * j)
                    res = x2f[:, c, bass.ds(j * BLK, BLK)]
                    nc.vector.scalar_tensor_tensor(x3f[:, c], pair_ps[c][:], INV, res, ALU.mult, ALU.add
                                                   ).then_inc(x3f_done, 1)
                for c in range(KT):
                    dve.wait_ge(x3hi_done, 2 * j + c + 1)
                    lo(x3s[:, 1, c], x3f[:, c], x3s[:, 0, c]).then_inc(x3lo_done, 1)

            dve.wait_ge(s_iota, BPG + 2)
            nc.vector.tensor_copy(pidx[:], iota_p[:])
            link(nc.vector.tensor_copy(pmod[:], iota_q[:]))
            link(nc.vector.tensor_scalar(eye32[:], iota_r[:, 0:C], pmod[:, 0:1], None, ALU.is_equal))
            dve.wait_ge(s_idx, 48)
            for n, rows in ((0, rows0), (1, rows1)):
                for q in range(BPG):
                    part = slice(q * C, (q + 1) * C)
                    nc.vector.tensor_scalar(rows[part, :], idx[part, n, :].rearrange("p (g b) -> p b g", b=BPG)[:, q, :],
                                            float(C), pmod[part, 0:1], ALU.mult, ALU.add).then_inc(s_rows, 1)
            nc.vector.tensor_scalar(ident[:], iota_r[:], pidx[:, 0:1], None, ALU.is_equal).then_inc(s_rows, 1)
            dve.wait_ge(s_small, 64)
            link(nc.vector.tensor_scalar(sel1[:], idx[:, 1, :], pmod[:, 0:1], None, ALU.is_equal))
            link(nc.vector.tensor_scalar(fhi[:], fraw[:], WS, None, ALU.mult))
            link(lo(fres[:], fraw[:], fhi[:], WS))
            link(nc.vector.tensor_copy(fmid[:], fres[:]))
            link(lo(flo[:], fres[:], fmid[:]))
            link(nc.vector.tensor_copy(fparts[:], fhi[:]))
            link(nc.vector.tensor_copy(fparts[C:2 * C, :], fmid[C:2 * C, :]))
            link(nc.vector.tensor_copy(fparts[2 * C:3 * C, :], flo[2 * C:3 * C, :]))
            bias_matrix(0)
            link(nc.vector.tensor_scalar(rel[:], idx[:, 1:3, :], -float(RANK), pidx[:, 0:1], ALU.mult, ALU.add))
            link(nc.vector.tensor_scalar(ge0[:], rel[:], 0.0, INV, ALU.is_ge, ALU.mult))
            nc.vector.scalar_tensor_tensor(mask2[:], rel[:, 0], float(RANK), ge0[:, 0], ALU.is_lt, ALU.mult)
            link(nc.vector.scalar_tensor_tensor(mask3[:], rel[:, 1], float(RANK), ge0[:, 1], ALU.is_lt, ALU.mult))
            link(nc.vector.tensor_scalar(mask3s[:], mask3[:], scol[:, 0:1], None, ALU.mult))

            dve.wait_ge(s_zero, 4)
            diagonals(0)
            weights_lo(0, 1)
            x2_copy(0)
            x2_lo(0)
            weights_lo(1, N_UP)
            body(0, True, False)
            with dve.Fori(1, NBLK - 1) as j:
                body(j, False, False)
            body(NBLK - 1, False, True)
            z3_mask(NBLK - 1)


_INS = ["x", "itok_B_1_198", "itok_B_0_7", "fside_8xS_0", "itok_B_0_6", "L0_cond_weights", "L1_cond_weights",
        "L2_cond_Wg", "L2_cond_Wu", "L2_cond_Wd", "L2_cond_Ag", "L2_cond_Bg", "L2_cond_Au", "L2_cond_Bu",
        "L2_cond_Ad", "L2_cond_Bd", "L3_cond_W", "L3_cond_A", "L3_cond_Bm", "L3_cond_scalings"]


def kernel(**inputs):
    import numpy as _np
    import concourse.bacc as _bacc
    from concourse.bass_utils import run_bass_kernel_spmd as _run

    nc = _bacc.Bacc("TRN2", target_bir_lowering=False, num_devices=1)
    arrays, args = {}, []
    for name in _INS:
        a = _np.ascontiguousarray(inputs[name])
        arrays[f"in_{name}"] = a
        args.append(nc.dram_tensor(f"in_{name}", a.shape, mybir.dt.from_np(a.dtype), kind="ExternalInput").ap())
    out = nc.dram_tensor("out_x", (B, C, T), mybir.dt.float32, kind="ExternalOutput").ap()
    build(nc, *args, out)
    return _run(nc, [arrays], core_ids=[0]).results[0]["out_x"]
```

```python
from contextlib import ExitStack

import concourse.bass as bass
from concourse import mybir

B, C, T = 128, 32, 256
NSEL, NAD, RANK, FF = 200, 8, 16, 1024
P = 128
NT = B * C
BLK = 512
NBLK = NT // BLK
GRP = BLK // P
BPG = P // C
BPB = BLK // C
KT = T // P
MF = FF // P
WS = 256.0
INV = 1.0 / WS
Q = 32
SLOTS = 2
GONE = -1000.0


def build(nc, x, i0, i1, bias, i3, w0, w1, wg, wu, wd, ag, bg, au, bu, ad, bd, w3, a3, bm, scal, out):
    f32, f16, i32, u32 = mybir.dt.float32, mybir.dt.float16, mybir.dt.int32, mybir.dt.uint32
    ALU, ACT = mybir.AluOpType, mybir.ActivationFunctionType

    w0_rows = w0.rearrange("s c d -> (s c) d")
    w1_rows = w1.rearrange("s c d -> (s c) d")
    x_rows = x.rearrange("b c t -> (b c) t")
    out_rows = out.rearrange("b c t -> (b c) t")
    wd_v = wd.rearrange("(p m) n -> p m n", m=MF)
    ad_v = ad.rearrange("n (p m) r -> p n (m r)", m=MF)

    with ExitStack() as ctx:
        def sb(name, shape, dt=f32):
            return ctx.enter_context(nc.sbuf_tensor(name, shape, dt))

        def sem(name):
            return ctx.enter_context(nc.semaphore(name))

        idx = sb("idx", [P, 3, B], i32)
        iota_p = sb("iota_p", [P, 1], i32)
        iota_q = sb("iota_q", [P, 1], i32)
        iota_r = sb("iota_r", [P, P], i32)
        pidx = sb("pidx", [P, 1])
        pmod = sb("pmod", [P, 1])
        ident = sb("ident", [P, P])
        eye32 = sb("eye32", [P, C])
        icol = sb("icol", [P, 3], i32)
        icolf = sb("icolf", [P, 4])
        vals = sb("vals", [P, 4, P], f16)
        own = sb("own", [P, NAD], f16)
        later = sb("later", [P, P], f16)
        one16 = sb("one16", [P, P], f16)
        tie = sb("tie", [P, NAD])
        left = sb("left", [P, NBLK, NAD])
        top = sb("top", [P, NBLK, 8])
        lack = sb("lack", [P, NBLK])
        step_l, step_s, step_v = (sb(n, [P, NAD]) for n in ("step_l", "step_s", "step_v"))
        prod = sb("prod", [P, NBLK, NAD])
        prod2 = sb("prod2", [P, NBLK, NAD])
        rank_all = sb("rank_all", [P, NAD])
        rank = sb("rank", [P, 1])
        mine = sb("mine", [P, NBLK])
        is_l, is_s = sb("is_l", [P, NBLK]), sb("is_s", [P, NBLK])
        prim_i, mine_i = sb("prim_i", [P, NBLK], i32), sb("mine_i", [P, NBLK], i32)
        prim_n, mine_n = sb("prim_n", [P, NBLK]), sb("mine_n", [P, NBLK])
        turn = sb("turn", [P, NBLK])
        base_i = sb("base_i", [P, NBLK])
        c1, c2, c3, c4 = (sb(n, [P, NBLK]) for n in ("c1", "c2", "c3", "c4"))
        slot = sb("slot", [P, 1])
        deal = sb("deal", [P, P], f16)
        perm = sb("perm", [P, 4, B])
        rows = sb("rows", [P, 3, NT // P], u32)
        rows_blk = sb("rows_blk", [P, 3, GRP], u32)
        rows_out = sb("rows_out", [P, GRP], u32)
        prim = sb("prim", [P, 1])
        rp = sb("rp", [P, 1])
        ad_p, ad_s, ad_x = (sb(n, [P, NBLK]) for n in ("ad_p", "ad_s", "ad_x"))
        ids = sb("ids", [1, SLOTS, NBLK], i32)
        rows_b = sb("rows_b", [P, NBLK], u32)
        rows_b_blk = sb("rows_b_blk", [P, 1], u32)
        first_p = sb("first_p", [P, NBLK, BPB])
        mask2 = sb("mask2", [P, B])
        rel = sb("rel", [P, B])
        ge0 = sb("ge0", [P, B])
        mask3 = sb("mask3", [P, B])
        mask3s = sb("mask3s", [P, B])
        scol = sb("scol", [P, 1])
        sel1 = sb("sel1", [P, B])
        fraw = sb("fraw", [P, C])
        fhi, fmid, flo, fparts = (sb(n, [P, C], f16) for n in ("fhi", "fmid", "flo", "fparts"))
        fres = sb("fres", [P, C])
        ones = sb("ones", [P, P], f16)

        wgu_raw = sb("wgu_raw", [P, 2, KT, FF])
        wd_raw = sb("wd_raw", [P, MF, T])
        agu_raw = sb("agu_raw", [P, 2, NAD, KT, RANK])
        ad_raw = sb("ad_raw", [P, NAD, MF, RANK])
        w3_raw = sb("w3_raw", [P, KT, T])
        w3_f = sb("w3_f", [P, KT, T])
        a3_raw = sb("a3_raw", [P, T])
        bm_raw = sb("bm_raw", [P, KT, NAD, RANK])
        ab3_f = sb("ab3_f", [P, 2, T])
        wgu = sb("wgu", [P, 2, 2, KT, MF, P], f16)
        wdd = sb("wdd", [P, 2, MF, T], f16)
        agu = sb("agu", [P, NAD, KT, 2, 2, RANK], f16)
        add = sb("add", [P, NAD, MF, 2, RANK], f16)
        w3t = sb("w3t", [P, 2, KT, T], f16)
        ab3 = sb("ab3", [P, 2, 2, T], f16)

        x0 = sb("x0", [P, GRP, T])
        agu_blk = sb("agu_blk", [P, KT, 4, SLOTS, RANK], f16)
        add_blk = sb("add_blk", [P, MF, 4, SLOTS, RANK], f16)
        bgu_got = sb("bgu_got", [P, 2, FF])
        bd_got = sb("bd_got", [P, T])
        bgu_blk = sb("bgu_blk", [P, 2, MF, P], f16)
        bd_blk = sb("bd_blk", [P, T], f16)
        got0 = sb("got0", [P, GRP, C])
        got1 = sb("got1", [P, GRP, C])
        diag0 = sb("diag0", [P, GRP, P])
        diag1 = sb("diag1", [P, GRP, P])
        x1 = sb("x1", [P, GRP, T])
        bias_rows = sb("bias_rows", [P, BLK], f16)
        x2f = sb("x2f", [P, KT, NT])
        x2s = sb("x2s", [P, 2, KT, BLK], f16)
        zf = sb("zf", [P, BLK])
        zg = sb("zg", [P, BLK], f16)
        zu = sb("zu", [P, BLK], f16)
        silu = sb("silu", [P, 2, BLK])
        hf = sb("hf", [P, 2, BLK])
        hs = sb("hs", [P, 2, MF, BLK], f16)
        zdf = sb("zdf", [P, BLK])
        zds = sb("zds", [P, BLK], f16)
        x3f = sb("x3f", [P, KT, BLK])
        x3s = sb("x3s", [P, 2, KT, BLK], f16)
        z3f = sb("z3f", [P, BLK])
        z3s = sb("z3s", [P, 2, BLK], f16)
        y = sb("y", [P, GRP, T])

        bank = [ctx.enter_context(nc.psum_tensor(f"bank{i}", [P, BLK], f32)) for i in range(8)]
        gate_ps, up_ps = bank[0:2], bank[2:4]
        za_ps, zb_ps = bank[4], bank[5]
        pair_ps = bank[6:8]

        s_idx, s_small, s_x0, s_y = sem("idx_loaded"), sem("small_loaded"), sem("x0_loaded"), sem("y_stored")
        s_w = {k: sem(f"{k}_loaded") for k in ("agu", "wgu0", "wgu1", "wd", "ad", "st3")}
        s_iota, s_rows, s_rowsblk, s_got, s_diag = (sem(n) for n in (
            "iota_done", "rows_done", "rows_blk_done", "rows_gathered", "diag_built"))
        s_zero, s_chain, s_const = sem("zeros_written"), sem("vector_chain"), sem("constants_done")
        s_icol, s_own, s_count, s_rank, s_deal, s_perm = (sem(n) for n in (
            "index_columns_loaded", "own_done", "counts_done", "ranks_done", "deal_done", "perm_done"))
        s_rowsb, s_bgot, s_bhi, s_blo, s_bdhi, s_bdlo, s_ablk, s_dblk, s_rowsout = (sem(n) for n in (
            "rows_b_copied", "b_gathered", "b_hi", "b_lo", "b_down_hi", "b_down_lo", "a_picked", "a_down_picked",
            "rows_out_copied"))
        s_wf, s_wlo = sem("wgu_scaled"), sem("wgu_lo")
        s_pre, s_hi, s_lo = sem("weights_scaled"), sem("weights_hi"), sem("weights_lo")
        s_t3, s_t3f = sem("transposed"), sem("transposed_copied")
        s_rb, s_ready = sem("bias_rows_done"), sem("gather_may_start")
        pe_x1, pe_x2, pe_z, pe_gate, pe_up, pe_zd, pe_d, pe_z3, pe_y = (sem(n) for n in (
            "pe_x1", "pe_x2", "pe_z", "pe_gate", "pe_up", "pe_zd", "pe_down", "pe_z3", "pe_y"))
        x1_done, x2f_done, x2hi_done, x2lo_done = sem("x1_done"), sem("x2f_done"), sem("x2hi_done"), sem("x2lo_done")
        zf_done, zhi_done, zlo_done = sem("zf_done"), sem("zhi_done"), sem("zlo_done")
        silu_done, hf_done, hhi_done, hlo_done = sem("silu_done"), sem("hf_done"), sem("hhi_done"), sem("hlo_done")
        zdf_done, zdhi_done, zdlo_done = sem("zdf_done"), sem("zdhi_done"), sem("zdlo_done")
        x3f_done, x3hi_done, x3lo_done = sem("x3f_done"), sem("x3hi_done"), sem("x3lo_done")
        z3f_done, z3hi_done, z3lo_done = sem("z3f_done"), sem("z3hi_done"), sem("z3lo_done")
        y_done = sem("y_done")

        def cols(ap):
            return ap.rearrange("p (c m) -> p m c", m=MF)

        SPLITS = [("agu", agu_raw[:, u].rearrange("p n k r -> p (n k) r"),
                   agu[:, :, :, u, 0, :].rearrange("p n k r -> p (n k) r"),
                   agu[:, :, :, u, 1, :].rearrange("p n k r -> p (n k) r")) for u in range(2)]
        N_A = len(SPLITS)
        SPLITS += [("ad", ad_raw[:].rearrange("p n m r -> p (n m) r"),
                    add[:, :, :, 0, :].rearrange("p n m r -> p (n m) r"),
                    add[:, :, :, 1, :].rearrange("p n m r -> p (n m) r")),
                   ("wd", wd_raw[:], wdd[:, 0], wdd[:, 1])]
        N_DOWN = len(SPLITS)
        N_ALL = N_DOWN + 2
        W_BYTES = {"agu": 16 * 2 * KT, "ad": 16, "wd": 16}

        def after(eng, s, value):
            if not (isinstance(value, int) and value <= 0):
                eng.wait_ge(s, value)

        block = ctx.enter_context(nc.Block())

        @block.sync
        def _(sp):
            for n, v in enumerate((i0, i1, i3)):
                sp.dma_start(icol[:, n:n + 1], v.rearrange("(b a) -> b a", a=1)).then_inc(s_icol, 16)
            for k in range(KT):
                for u, w in enumerate((wg, wu)):
                    sp.dma_start(wgu_raw[:, u, k, :], w[k * P:(k + 1) * P, :]).then_inc(s_w[f"wgu{k}"], 16)
            sp.dma_start(wd_raw[:], wd_v).then_inc(s_w["wd"], 16)

        @block.gpsimd
        def _(pool):
            nc.gpsimd.memset(fraw[:], 0.0).then_inc(s_zero, 1)
            nc.gpsimd.iota(iota_p[:], pattern=[[0, 1]], base=0, channel_multiplier=1).then_inc(s_iota, 1)
            for q in range(BPG):
                pool.wait_ge(s_iota, q + 1)
                nc.gpsimd.iota(iota_q[q * C:(q + 1) * C, :], pattern=[[0, 1]], base=0,
                               channel_multiplier=1).then_inc(s_iota, 1)
            pool.wait_ge(s_iota, BPG + 1)
            nc.gpsimd.iota(iota_r[:], pattern=[[1, P]], base=0, channel_multiplier=0).then_inc(s_iota, 1)
            nc.gpsimd.memset(diag0[:], 0.0).then_inc(s_zero, 1)
            nc.gpsimd.memset(diag1[:], 0.0).then_inc(s_zero, 1)
            nc.gpsimd.memset(ones[:], INV).then_inc(s_zero, 1)
            nc.gpsimd.memset(one16[:], 1.0).then_inc(s_zero, 1)
            for a in range(NAD):
                nc.gpsimd.memset(tie[:, a:a + 1], 2.0 ** -(4 + a)).then_inc(s_zero, 1)
            for k in range(KT):
                for u in range(2):
                    pool.wait_ge(s_wf, 2 * (2 * k + u + 1))
                    nc.gpsimd.tensor_tensor(wgu[:, 1, u, k], cols(wgu_raw[:, u, k, :]), wgu[:, 0, u, k],
                                            ALU.subtract).then_inc(s_wlo, 1)

            def gather_x(b):
                nc.gpsimd.tensor_copy(rows_blk[:], rows[:, :, bass.ds(b * GRP, GRP)]).then_inc(s_rowsblk, 1)
                pool.wait_ge(s_rowsblk, b + 1)
                pool.sem_inc(s_ready, 1)
                for g in range(GRP):
                    for n, (table, got) in enumerate(((w0_rows, got0), (w1_rows, got1), (x_rows, x0))):
                        nc.gpsimd.indirect_dma_start(
                            out=got[:, g, :], out_offset=None, in_=table,
                            in_offset=bass.IndirectOffsetOnAxis(ap=rows_blk[:, n, g:g + 1], axis=0)
                        ).then_inc(s_x0 if n == 2 else s_got, 16)

            def gather_b(b):
                nc.gpsimd.tensor_copy(rows_b_blk[:], rows_b[:, bass.ds(b, 1)]).then_inc(s_rowsb, 1)
                pool.wait_ge(s_rowsb, b + 1)
                pool.sem_inc(s_ready, 1)
                for table, got in ((bg, bgu_got[:, 0, :]), (bu, bgu_got[:, 1, :]), (bd, bd_got[:])):
                    nc.gpsimd.indirect_dma_start(
                        out=got, out_offset=None, in_=table.rearrange("n r f -> (n r) f"),
                        in_offset=bass.IndirectOffsetOnAxis(ap=rows_b_blk[:, 0:1], axis=0)).then_inc(s_bgot, 16)

            def scatter_y(b):
                nc.gpsimd.tensor_copy(rows_out[:], rows[:, 2, bass.ds(b * GRP, GRP)]).then_inc(s_rowsout, 1)
                pool.wait_ge(s_rowsout, b + 1)
                pool.wait_ge(y_done, 2 * b + 2)
                pool.sem_inc(s_ready, 1)
                for g in range(GRP):
                    nc.gpsimd.indirect_dma_start(
                        out=out_rows, out_offset=bass.IndirectOffsetOnAxis(ap=rows_out[:, g:g + 1], axis=0),
                        in_=y[:, g, :], in_offset=None).then_inc(s_y, 16)

            def next_gathers(j):
                pool.wait_ge(s_diag, 8 * (j + 1))
                pool.wait_ge(pe_x1, 2 * (j + 1))
                pool.sem_inc(s_ready, 1)
                gather_x(j + 1)
                pool.wait_ge(s_blo, 2 * (j + 1))
                pool.wait_ge(s_bdlo, j + 1)
                pool.sem_inc(s_ready, 1)
                gather_b(j + 1)

            pool.wait_ge(s_rows, BPG)
            gather_x(0)
            pool.wait_ge(s_rows, BPG + 1)
            gather_b(0)
            next_gathers(0)
            with pool.Fori(1, NBLK - 1) as j:
                next_gathers(j)
                scatter_y(j - 1)
                pool.wait_ge(s_y, 16 * GRP * j)
                pool.sem_inc(s_ready, 1)
            scatter_y(NBLK - 2)
            pool.wait_ge(s_y, 16 * GRP * (NBLK - 1))
            scatter_y(NBLK - 1)
            pool.wait_ge(s_y, 16 * GRP * NBLK)

        @block.tensor
        def _(pe):
            def three(ps, whi, wlo, vhi, vlo, start, stop):
                nc.tensor.matmul(ps, whi, vhi, start=start, stop=False)
                nc.tensor.matmul(ps, wlo, vhi, start=False, stop=False)
                return nc.tensor.matmul(ps, whi, vlo, start=False, stop=stop)

            def mix0(b):
                pe.wait_ge(s_x0, 16 * GRP * (b + 1))
                pe.wait_ge(s_diag, 8 * (b + 1))
                for g in range(GRP):
                    last = nc.tensor.matmul(pair_ps[g // 2][:, (g % 2) * T:(g % 2 + 1) * T], diag0[:, g, :],
                                            x0[:, g, :], start=True, stop=True)
                    if g % 2:
                        last.then_inc(pe_x1, 1)

            def mix1(b):
                pe.wait_ge(x1_done, 2 * (b + 1))
                pe.wait_ge(s_rb, b + 1)
                for k in range(KT):
                    nc.tensor.matmul(pair_ps[k][:], ones[:], bias_rows[:], start=True, stop=False)
                    for g in range(GRP):
                        last = nc.tensor.matmul(pair_ps[k][:, g * P:(g + 1) * P], x1[:, g, k * P:(k + 1) * P],
                                                diag1[:, g, :], start=False, stop=g == GRP - 1)
                    last.then_inc(pe_x2, 1)

            def lora3(b):
                pe.wait_ge(x3lo_done, 2 * (b + 1))
                for k in range(KT):
                    cut = slice(k * P, (k + 1) * P)
                    last = three(zb_ps[:], ab3[:, 0, 0, cut], ab3[:, 1, 0, cut], x3s[:, 0, k], x3s[:, 1, k],
                                 k == 0, k == KT - 1)
                last.then_inc(pe_z3, 1)

            def out3(b):
                pe.wait_ge(z3lo_done, b + 1)
                for g in range(GRP):
                    cut = slice(g * P, (g + 1) * P)
                    ps = pair_ps[g // 2][:, (g % 2) * T:(g % 2 + 1) * T]
                    for k in range(KT):
                        three(ps, x3s[:, 0, k, cut], x3s[:, 1, k, cut], w3t[:, 0, k], w3t[:, 1, k], k == 0, False)
                    last = three(ps, z3s[:, 0, cut], z3s[:, 1, cut], ab3[:, 0, 1], ab3[:, 1, 1], False, True)
                    if g % 2:
                        last.then_inc(pe_y, 1)

            def body(j, first, last_block):
                pe.wait_ge(x2lo_done, 2 * (j + 1))
                pe.wait_ge(s_ablk, 2 * (j + 1))
                if not first:
                    pe.wait_ge(zdf_done, j)
                for k in range(KT):
                    for h in range(2):
                        last = nc.tensor.matmul(za_ps[:], agu_blk[:, k].rearrange("p q s r -> p (q s r)"),
                                                x2s[:, h, k], start=k + h == 0, stop=k + h == KT)
                last.then_inc(pe_z, 1)
                if first:
                    pe.wait_ge(s_wlo, 2 * KT)

                def dense(m):
                    if not first or m >= 2:
                        pe.wait_ge(silu_done, 8 * j + m - 1)
                        pe.wait_ge(hf_done, 8 * j + m - 1)
                    for u, ps in enumerate((gate_ps[m % 2], up_ps[m % 2])):
                        for k in range(KT):
                            three(ps[:], wgu[:, 0, u, k, m], wgu[:, 1, u, k, m], x2s[:, 0, k], x2s[:, 1, k],
                                  k == 0, False)

                def lora(m):
                    nc.tensor.matmul(gate_ps[m % 2][:], bgu_blk[:, 0, m], zg[:], start=False, stop=True
                                     ).then_inc(pe_gate, 1)
                    nc.tensor.matmul(up_ps[m % 2][:], bgu_blk[:, 1, m], zu[:], start=False, stop=True
                                     ).then_inc(pe_up, 1)

                for m in range(MF):
                    if m != 1:
                        dense(m)
                    if m == 0:
                        dense(1)
                        pe.wait_ge(zhi_done, 4 * (j + 1))
                        pe.wait_ge(zlo_done, 2 * (j + 1))
                        pe.wait_ge(s_blo, 2 * (j + 1))
                    lora(m)
                    if m == 1 and first:
                        pe.wait_ge(s_w["st3"], 16 * 4)
                        for k in range(KT):
                            nc.tensor.transpose(zb_ps[:, k * P:(k + 1) * P], a3_raw[:, k * P:(k + 1) * P], ident[:])
                            last = nc.tensor.transpose(zb_ps[:, T + k * P:T + (k + 1) * P],
                                                       bm_raw[:, k].rearrange("p n r -> p (n r)"), ident[:])
                        last.then_inc(s_t3, 1)
                        for k in range(KT):
                            for o in range(KT):
                                last = nc.tensor.transpose(pair_ps[0][:, k * T + o * P:k * T + (o + 1) * P],
                                                           w3_raw[:, o, k * P:(k + 1) * P], ident[:])
                        last.then_inc(s_t3, 1)
                    if m == 1 and not first:
                        lora3(j - 1)
                    if m == 3 and not first:
                        out3(j - 1)
                    if m == 5 and not last_block:
                        if first:
                            pe.wait_ge(s_t3f, 3)
                        else:
                            pe.wait_ge(y_done, 2 * j)
                        mix0(j + 1)
                if not last_block:
                    mix1(j + 1)
                if first:
                    pe.wait_ge(s_lo, N_DOWN)
                pe.wait_ge(s_dblk, 4 * (j + 1))
                pe.wait_ge(hlo_done, 8 * (j + 1))
                for m in range(MF):
                    for h in range(2):
                        last = nc.tensor.matmul(za_ps[:], add_blk[:, m].rearrange("p q s r -> p (q s r)"),
                                                hs[:, h, m], start=m + h == 0, stop=m + h == MF)
                last.then_inc(pe_zd, 1)
                if last_block:
                    pe.wait_ge(y_done, 2 * j)
                else:
                    pe.wait_ge(x2f_done, 2 * (j + 2))
                for c in range(KT):
                    cut = slice(c * P, (c + 1) * P)
                    for m in range(MF):
                        three(pair_ps[c][:], wdd[:, 0, m, cut], wdd[:, 1, m, cut], hs[:, 0, m], hs[:, 1, m],
                              m == 0, False)
                pe.wait_ge(zdlo_done, j + 1)
                pe.wait_ge(s_bdlo, j + 1)
                for c in range(KT):
                    cut = slice(c * P, (c + 1) * P)
                    nc.tensor.matmul(pair_ps[c][:], bd_blk[:, cut], zds[:], start=False, stop=True
                                     ).then_inc(pe_d, 1)

            pe.wait_ge(s_zero, 5)
            pe.wait_ge(s_own, 1)
            nc.tensor.matmul(zb_ps[:, 0:NAD], one16[:], own[:], start=True, stop=True).then_inc(s_count, 1)
            nc.tensor.matmul(za_ps[:, 0:NAD], later[:], own[:], start=True, stop=True).then_inc(s_rank, 1)
            pe.wait_ge(s_deal, 1)
            for n in range(4):
                last = nc.tensor.matmul(zb_ps[:, n * P:(n + 1) * P], vals[:, n, :], deal[:], start=True, stop=True)
            last.then_inc(s_perm, 1)
            mix0(0)
            mix1(0)
            body(0, True, False)
            pe.wait_ge(s_lo, N_ALL)
            with pe.Fori(1, NBLK - 1) as j:
                body(j, False, False)
            body(NBLK - 1, False, True)
            lora3(NBLK - 1)
            out3(NBLK - 1)

        @block.scalar
        def _(act):
            def half(dst, src, scale=1.0):
                return nc.scalar.activation(dst, src, ACT.Copy, scale=scale)

            act.wait_ge(s_zero, 1)
            for q in range(3):
                act.dma_start(fraw[q * C:q * C + NAD, :], bias).then_inc(s_small, 16)
            act.dma_start(scol[:], scal.rearrange("(n a) -> n a", a=1).unsqueeze(1).to_broadcast([NAD, RANK, 1])
                          ).then_inc(s_small, 16)
            for u, a in enumerate((ag, au)):
                for k in range(KT):
                    act.dma_start(agu_raw[:, u, :, k, :], a[:, k * P:(k + 1) * P, :].rearrange("n p r -> p n r")
                                  ).then_inc(s_w["agu"], 16)
            act.dma_start(ad_raw[:].rearrange("p n m r -> p n (m r)"), ad_v).then_inc(s_w["ad"], 16)
            act.dma_start(w3_raw[:], w3.rearrange("(o p) i -> p o i", p=P)).then_inc(s_w["st3"], 16)
            act.dma_start(a3_raw[:], a3.rearrange("n r i -> (n r) i")).then_inc(s_w["st3"], 16)
            for k in range(KT):
                act.dma_start(bm_raw[:, k], bm[:, k * P:(k + 1) * P, :].rearrange("n p r -> p n r")
                              ).then_inc(s_w["st3"], 16)

            def x1_copy(b):
                for h in range(2):
                    act.wait_ge(pe_x1, 2 * b + h + 1)
                    half(x1[:, 2 * h:2 * h + 2, :].rearrange("p g t -> p (g t)"), pair_ps[h][:]).then_inc(x1_done, 1)

            def x2_hi(b):
                for k in range(KT):
                    act.wait_ge(x2f_done, 2 * b + k + 1)
                    half(x2s[:, 0, k], x2f[:, k, bass.ds(b * BLK, BLK)]
                         ).then_inc(x2hi_done, 1)

            def y_copy(b):
                for h in range(2):
                    act.wait_ge(pe_y, 2 * b + h + 1)
                    half(y[:, 2 * h:2 * h + 2, :].rearrange("p g t -> p (g t)"), pair_ps[h][:], INV
                         ).then_inc(y_done, 1)

            def z3_hi(b):
                act.wait_ge(z3f_done, b + 1)
                half(z3s[:, 0], z3f[:]).then_inc(z3hi_done, 1)

            def weights_hi(a, b):
                for name, src, hi, _ in SPLITS[a:b]:
                    act.wait_ge(s_w[name], W_BYTES[name])
                    half(hi, src, WS).then_inc(s_hi, 1)

            def b_hi(b):
                act.wait_ge(s_bgot, 48 * (b + 1))
                for u in range(2):
                    half(bgu_blk[:, u], cols(bgu_got[:, u, :]), WS).then_inc(s_bhi, 1)

            def h_hi(j, m):
                act.wait_ge(hf_done, 8 * j + m + 1)
                half(hs[:, 0, m], hf[:, m % 2]).then_inc(hhi_done, 1)

            def body(j, first, last_block):
                act.wait_ge(zf_done, j + 1)
                half(zg[0:2 * Q], zf[0:2 * Q]).then_inc(zhi_done, 1)
                half(zu[2 * Q:4 * Q], zf[2 * Q:4 * Q]).then_inc(zhi_done, 1)
                half(zg[3 * Q:4 * Q], zf[0:Q]).then_inc(zhi_done, 1)
                half(zu[Q:2 * Q], zf[2 * Q:3 * Q]).then_inc(zhi_done, 1)
                if first:
                    weights_hi(N_A, N_DOWN)
                for m in range(MF):
                    act.wait_ge(pe_gate, 8 * j + m + 1)
                    nc.scalar.activation(silu[:, m % 2], gate_ps[m % 2][:], ACT.Silu, scale=INV
                                         ).then_inc(silu_done, 1)
                    if m:
                        h_hi(j, m - 1)
                    if m == 2 and not first:
                        z3_hi(j - 1)
                    if m == 2 and first:
                        act.wait_ge(s_t3f, 1)
                        half(ab3[:, 0], ab3_f[:], WS).then_inc(s_hi, 1)
                        act.wait_ge(s_t3f, 3)
                        half(w3t[:, 0], w3_f[:], WS).then_inc(s_hi, 1)
                    if m == 4 and not first:
                        y_copy(j - 1)
                    if m == 5:
                        half(bd_blk[:], bd_got[:], WS).then_inc(s_bdhi, 1)
                    if m == 6 and not last_block:
                        x1_copy(j + 1)
                h_hi(j, MF - 1)
                if not last_block:
                    x2_hi(j + 1)
                act.wait_ge(zdf_done, j + 1)
                half(zds[:], zdf[:]).then_inc(zdhi_done, 1)
                if not last_block:
                    b_hi(j + 1)
                for c in range(KT):
                    act.wait_ge(x3f_done, 2 * j + c + 1)
                    half(x3s[:, 0, c], x3f[:, c]).then_inc(x3hi_done, 1)
                if not first:
                    act.wait_ge(s_y, 16 * GRP * j)

            weights_hi(0, N_A)
            for k in range(KT):
                act.wait_ge(s_w[f"wgu{k}"], 32)
                for u in range(2):
                    raw = wgu_raw[:, u, k, :]
                    half(raw, raw, WS).then_inc(s_wf, 1)
                    act.wait_ge(s_wf, 4 * k + 2 * u + 1)
                    half(wgu[:, 0, u, k], cols(raw)).then_inc(s_wf, 1)
            x1_copy(0)
            x2_hi(0)
            b_hi(0)
            body(0, True, False)
            with act.Fori(1, NBLK - 1) as j:
                body(j, False, False)
            body(NBLK - 1, False, True)
            z3_hi(NBLK - 1)
            y_copy(NBLK - 1)

        @block.vector
        def _(dve):
            chain = [0]

            def link(ins):
                chain[0] += 1
                ins.then_inc(s_chain, 1)
                dve.wait_ge(s_chain, chain[0])

            def lo(dst, src, hi, scale=1.0):
                if scale == 1.0:
                    return nc.vector.tensor_tensor(dst, src, hi, ALU.subtract)
                return nc.vector.scalar_tensor_tensor(dst, src, scale, hi, ALU.mult, ALU.subtract)

            def by_batch(ap, b):
                return ap[:, bass.ds(b * BPB, BPB)].unsqueeze(2).to_broadcast([P, BPB, C])

            def tokens(ap):
                return ap.rearrange("p (b c) -> p b c", c=C)

            def bias_matrix(b):
                nc.vector.tensor_tensor(tokens(bias_rows[:]), fparts[:].unsqueeze(1).to_broadcast([P, BPB, C]),
                                        by_batch(sel1, b), ALU.mult).then_inc(s_rb, 1)

            def diagonals(b):
                dve.wait_ge(s_got, 16 * 2 * GRP * (b + 1))
                for got, diag in ((got0, diag0), (got1, diag1)):
                    for q in range(BPG):
                        rows = slice(q * C, (q + 1) * C)
                        nc.vector.tensor_tensor(
                            diag[rows, :, rows], got[rows, :, :],
                            eye32[rows, :].unsqueeze(1).to_broadcast([C, GRP, C]), ALU.add).then_inc(s_diag, 1)

            def x2_copy(b):
                for k in range(KT):
                    dve.wait_ge(pe_x2, 2 * b + k + 1)
                    dst = x2f[:, k, bass.ds(b * BLK, BLK)]
                    nc.vector.tensor_copy(dst, pair_ps[k][:]).then_inc(x2f_done, 1)

            def x2_lo(b):
                for k in range(KT):
                    dve.wait_ge(x2hi_done, 2 * b + k + 1)
                    src = x2f[:, k, bass.ds(b * BLK, BLK)]
                    lo(x2s[:, 1, k], src, x2s[:, 0, k]).then_inc(x2lo_done, 1)

            def z3_mask(b):
                dve.wait_ge(pe_z3, b + 1)
                nc.vector.tensor_tensor(tokens(z3f[:]), tokens(zb_ps[:]), by_batch(mask3s, b), ALU.mult
                                        ).then_inc(z3f_done, 1)
                dve.wait_ge(z3hi_done, b + 1)
                lo(z3s[:, 1], z3f[:], z3s[:, 0]).then_inc(z3lo_done, 1)
                dve.wait_ge(z3lo_done, b + 1)

            def weights_lo(a, b):
                for n, (_, src, hi, low) in enumerate(SPLITS[a:b], a):
                    dve.wait_ge(s_hi, n + 1)
                    lo(low, src, hi, WS).then_inc(s_lo, 1)

            def b_lo(b):
                for u, q in ((0, 3), (1, 1)):
                    part = slice(q * Q, (q + 1) * Q)
                    dve.wait_ge(s_bhi, 2 * b + u + 1)
                    lo(bgu_blk[part, u], cols(bgu_got[part, u, :]), bgu_blk[part, u], WS).then_inc(s_blo, 1)

            def pick(b, table, blk, done):
                for s in range(SLOTS):
                    a = dve.value_load(ids[0:1, s, bass.ds(b, 1)], min_val=0, max_val=NAD - 1)
                    src = table[:, bass.ds(a, 1)]
                    if table is agu:
                        nc.vector.tensor_copy(blk[:, :, :, s, :].rearrange("p k q r -> p (k q) r"),
                                              src.rearrange("p n k u h r -> p (n k u h) r")).then_inc(done, 1)
                    else:
                        src = src.rearrange("p n m h r -> p (n m) h r")
                        nc.vector.tensor_copy(blk[:, :, 0:2, s, :], src).then_inc(done, 1)
                        nc.vector.tensor_copy(blk[:, :, 2:4, s, :], src[:, :, 0:1, :].to_broadcast([P, MF, 2, RANK])
                                              ).then_inc(done, 1)

            def h_lo(j, m):
                dve.wait_ge(hhi_done, 8 * j + m + 1)
                lo(hs[:, 1, m], hf[:, m % 2], hs[:, 0, m]).then_inc(hlo_done, 1)

            def body(j, first, last_block):
                dve.wait_ge(pe_z, j + 1)
                after(dve, zlo_done, 2 * j)
                nc.vector.tensor_tensor(tokens(zf[:]), tokens(za_ps[:]), by_batch(mask2, j), ALU.mult
                                        ).then_inc(zf_done, 1)
                dve.wait_ge(zhi_done, 4 * (j + 1))
                lo(zg[2 * Q:3 * Q], zf[0:Q], zg[0:Q]).then_inc(zlo_done, 1)
                lo(zu[0:Q], zf[2 * Q:3 * Q], zu[2 * Q:3 * Q]).then_inc(zlo_done, 1)
                if first:
                    weights_lo(N_A, N_DOWN)
                    dve.wait_ge(s_lo, N_A + 1)
                    pick(0, add, add_blk, s_dblk)
                for m in range(MF):
                    dve.wait_ge(silu_done, 8 * j + m + 1)
                    dve.wait_ge(pe_up, 8 * j + m + 1)
                    if not first or m >= 2:
                        dve.wait_ge(hlo_done, 8 * j + m - 1)
                    nc.vector.scalar_tensor_tensor(hf[:, m % 2], up_ps[m % 2][:], INV, silu[:, m % 2],
                                                   ALU.mult, ALU.mult).then_inc(hf_done, 1)
                    if m:
                        h_lo(j, m - 1)
                    if m == 3 and not last_block:
                        bias_matrix(j + 1)
                        diagonals(j + 1)
                    if m == 6:
                        dve.wait_ge(s_bdhi, j + 1)
                        lo(bd_blk[3 * Q:], bd_got[3 * Q:], bd_blk[3 * Q:], WS).then_inc(s_bdlo, 1)
                    if m == 2 and not first:
                        z3_mask(j - 1)
                    if m == 2 and first:
                        dve.wait_ge(s_t3, 1)
                        nc.vector.tensor_copy(ab3_f[:].rearrange("p a t -> p (a t)"), zb_ps[:]).then_inc(s_t3f, 1)
                        dve.wait_ge(s_t3, 2)
                        for k in range(KT):
                            other = slice((1 - k) * P, (2 - k) * P)
                            link(nc.vector.tensor_copy(w3_f[:, k, other], pair_ps[0][:, k * T + (1 - k) * P:
                                                                                     k * T + (2 - k) * P]))
                            nc.vector.tensor_tensor(w3_f[:, k, k * P:(k + 1) * P],
                                                    pair_ps[0][:, k * T + k * P:k * T + (k + 1) * P],
                                                    ident[:], ALU.add).then_inc(s_t3f, 1)
                        dve.wait_ge(s_hi, N_DOWN + 1)
                        lo(ab3[:, 1], ab3_f[:], ab3[:, 0], WS).then_inc(s_lo, 1)
                        dve.wait_ge(s_hi, N_DOWN + 2)
                        lo(w3t[:, 1], w3_f[:], w3t[:, 0], WS).then_inc(s_lo, 1)
                h_lo(j, MF - 1)
                if not last_block:
                    x2_copy(j + 1)
                    x2_lo(j + 1)
                dve.wait_ge(pe_zd, j + 1)
                after(dve, zdlo_done, j)
                nc.vector.tensor_tensor(tokens(zdf[:]), tokens(za_ps[:]), by_batch(mask2, j), ALU.mult
                                        ).then_inc(zdf_done, 1)
                dve.wait_ge(zdhi_done, j + 1)
                lo(zds[2 * Q:3 * Q], zdf[2 * Q:3 * Q], zds[2 * Q:3 * Q]).then_inc(zdlo_done, 1)
                if not last_block:
                    pick(j + 1, agu, agu_blk, s_ablk)
                    pick(j + 1, add, add_blk, s_dblk)
                    b_lo(j + 1)
                for c in range(KT):
                    dve.wait_ge(pe_d, 2 * j + c + 1)
                    after(dve, x3lo_done, 2 * j)
                    res = x2f[:, c, bass.ds(j * BLK, BLK)]
                    nc.vector.scalar_tensor_tensor(x3f[:, c], pair_ps[c][:], INV, res, ALU.mult, ALU.add
                                                   ).then_inc(x3f_done, 1)
                for c in range(KT):
                    dve.wait_ge(x3hi_done, 2 * j + c + 1)
                    lo(x3s[:, 1, c], x3f[:, c], x3s[:, 0, c]).then_inc(x3lo_done, 1)

            def tsc(out, src, a, b, op0, op1=None):
                return nc.vector.tensor_scalar(out, src, a, b, op0) if op1 is None else \
                    nc.vector.tensor_scalar(out, src, a, b, op0, op1)

            def over_slots(ap):
                return ap.unsqueeze(2).to_broadcast([P, NBLK, BPB])

            def over_blocks(ap):
                return ap.unsqueeze(1).to_broadcast([P, NBLK, NAD])

            def over_adapters(ap):
                return ap.unsqueeze(2).to_broadcast([P, NBLK, NAD])

            dve.wait_ge(s_iota, BPG + 2)
            nc.vector.tensor_copy(pidx[:], iota_p[:]).then_inc(s_chain, 1)
            chain[0] += 1
            link(nc.vector.tensor_copy(pmod[:], iota_q[:]))
            nc.vector.tensor_copy(icolf[:, 2:3], iota_p[:])
            link(tsc(later[:], iota_r[:], pidx[:, 0:1], None, ALU.is_gt))
            dve.wait_ge(s_icol, 48)
            nc.vector.tensor_copy(icolf[:, 0:2], icol[:, 0:2])
            link(nc.vector.tensor_copy(icolf[:, 3:4], icol[:, 2:3]))
            tsc(own[:], iota_r[:, 0:NAD], icolf[:, 1:2], None, ALU.is_equal).then_inc(s_own, 1)
            nc.vector.tensor_copy(vals[:], icolf[:].unsqueeze(2).to_broadcast([P, 4, P]))
            tsc(ident[:], iota_r[:], pidx[:, 0:1], None, ALU.is_equal)
            tsc(eye32[:], iota_r[:, 0:C], pmod[:, 0:1], None, ALU.is_equal)
            link(tsc(base_i[:], iota_r[:, 0:NBLK], float(BPB), None, ALU.mult))
            dve.wait_ge(s_zero, 5 + NAD)
            dve.wait_ge(s_count, 1)
            link(nc.vector.tensor_tensor(left[:, 0, :], zb_ps[:, 0:NAD], tie[:], ALU.add))
            for i in range(NBLK):
                most, fewest = top[:, i, 0:1], top[:, i, 7 - i:8 - i]
                link(nc.vector.max(top[:, i, :], left[:, i, :]))
                link(tsc(lack[:, i:i + 1], fewest, -float(BPB), None, ALU.add))
                if i < NBLK - 1:
                    tsc(step_s[:], left[:, i, :], fewest, GONE, ALU.is_equal, ALU.mult)
                    link(tsc(step_l[:], left[:, i, :], most, lack[:, i:i + 1], ALU.is_equal, ALU.mult))
                    link(nc.vector.tensor_tensor(step_v[:], step_l[:], step_s[:], ALU.add))
                    link(nc.vector.tensor_tensor(left[:, i + 1, :], left[:, i, :], step_v[:], ALU.add))
            tops = top[:].rearrange("p i a -> p (i a)")
            most, fewest = tops[:, 0:NBLK * 8:8], tops[:, 7:7 * NBLK + 1:7]
            dve.wait_ge(s_rank, 1)
            nc.vector.tensor_tensor(rank_all[:], za_ps[:, 0:NAD], own[:], ALU.mult)
            nc.vector.tensor_copy(prim_i[:], fewest)
            link(nc.vector.tensor_tensor(prod[:], left[:], over_blocks(own[:]), ALU.mult))
            nc.vector.reduce_sum(rank[:], rank_all[:], axis=mybir.AxisListType.X)
            link(nc.vector.reduce_sum(mine[:], prod[:], axis=mybir.AxisListType.X))
            nc.vector.tensor_tensor(is_l[:], mine[:], most, ALU.is_equal)
            nc.vector.tensor_tensor(is_s[:], mine[:], fewest, ALU.is_equal)
            nc.vector.tensor_copy(mine_i[:], mine[:])
            link(nc.vector.tensor_copy(prim_n[:], prim_i[:]))
            link(nc.vector.tensor_copy(mine_n[:], mine_i[:]))
            link(tsc(turn[:], mine_n[:], mine_n[:, 0:1], rank[:, 0:1], ALU.subtract, ALU.add))
            link(tsc(c1[:], turn[:], 0.0, None, ALU.is_ge))
            link(nc.vector.tensor_tensor(c2[:], turn[:], prim_n[:], ALU.add))
            link(nc.vector.scalar_tensor_tensor(c3[:], c2[:], float(BPB), is_l[:], ALU.is_lt, ALU.mult))
            nc.vector.tensor_tensor(c2[:], c2[:], base_i[:], ALU.add)
            link(nc.vector.tensor_tensor(c4[:], turn[:], base_i[:], ALU.add))
            nc.vector.tensor_tensor(c3[:], c3[:], c2[:], ALU.mult)
            link(nc.vector.tensor_tensor(c4[:], c4[:], is_s[:], ALU.mult))
            link(nc.vector.tensor_tensor(c3[:], c3[:], c4[:], ALU.add))
            link(nc.vector.tensor_tensor(c3[:], c3[:], c1[:], ALU.mult))
            link(nc.vector.reduce_sum(slot[:], c3[:], axis=mybir.AxisListType.X))
            tsc(deal[:], iota_r[:], slot[:, 0:1], None, ALU.is_equal).then_inc(s_deal, 1)
            tsc(prim[:], pmod[:], float(RANK), None, ALU.is_lt)
            link(nc.vector.tensor_tensor(prod[:], left[:], over_adapters(fewest), ALU.is_equal))
            nc.vector.tensor_tensor(prod2[:], left[:], over_adapters(most), ALU.is_equal)
            nc.vector.tensor_tensor(prod[:], prod[:], over_blocks(iota_r[:, 0:NAD]), ALU.mult)
            link(tsc(rp[:], prim[:], float(RANK), pmod[:, 0:1], ALU.mult, ALU.add))
            link(nc.vector.tensor_tensor(prod2[:], prod2[:], over_blocks(iota_r[:, 0:NAD]), ALU.mult))
            nc.vector.reduce_sum(ad_p[:], prod[:], axis=mybir.AxisListType.X)
            link(nc.vector.reduce_sum(ad_s[:], prod2[:], axis=mybir.AxisListType.X))
            nc.vector.tensor_copy(ids[0:1, 0, :], ad_p[0:1, :])
            nc.vector.tensor_copy(ids[0:1, 1, :], ad_s[0:1, :])
            link(nc.vector.tensor_tensor(ad_x[:], ad_p[:], ad_s[:], ALU.subtract))
            link(nc.vector.scalar_tensor_tensor(ad_x[:], ad_x[:], prim[:, 0:1], ad_s[:], ALU.mult, ALU.add))
            link(tsc(ad_x[:], ad_x[:], float(RANK), -float(RANK), ALU.mult, ALU.add))
            dve.wait_ge(s_perm, 1)
            link(nc.vector.tensor_copy(perm[:].rearrange("p n b -> p (n b)"), zb_ps[:]))
            for q in range(BPG):
                part = slice(q * C, (q + 1) * C)
                tsc(rows[part], perm[part, 0:3, :].rearrange("p n (g b) -> p n b g", b=BPG)[:, :, q, :],
                    float(C), pmod[part, 0:1], ALU.mult, ALU.add).then_inc(s_rows, 1)
            tsc(rows_b[:], ad_x[:], rp[:, 0:1], None, ALU.add).then_inc(s_rows, 1)
            dve.wait_ge(s_small, 64)
            tsc(sel1[:], perm[:, 1, :], pmod[:, 0:1], None, ALU.is_equal)
            link(tsc(fhi[:], fraw[:], WS, None, ALU.mult))
            link(lo(fres[:], fraw[:], fhi[:], WS))
            link(nc.vector.tensor_copy(fmid[:], fres[:]))
            link(lo(flo[:], fres[:], fmid[:]))
            link(nc.vector.tensor_copy(fparts[:], fhi[:]))
            link(nc.vector.tensor_copy(fparts[C:2 * C, :], fmid[C:2 * C, :]))
            link(nc.vector.tensor_copy(fparts[2 * C:3 * C, :], flo[2 * C:3 * C, :]))
            bias_matrix(0)
            link(nc.vector.tensor_tensor(first_p[:], iota_r[:, 0:BPB].unsqueeze(1).to_broadcast([P, NBLK, BPB]), over_slots(prim_n[:]), ALU.is_lt))
            tsc(mask2[:], first_p[:].rearrange("p i t -> p (i t)"), prim[:, 0:1], INV, ALU.is_equal, ALU.mult)
            link(tsc(rel[:], perm[:, 3, :], -float(RANK), pidx[:, 0:1], ALU.mult, ALU.add))
            link(tsc(ge0[:], rel[:], 0.0, INV, ALU.is_ge, ALU.mult))
            link(nc.vector.scalar_tensor_tensor(mask3[:], rel[:], float(RANK), ge0[:], ALU.is_lt, ALU.mult))
            link(tsc(mask3s[:], mask3[:], scol[:, 0:1], None, ALU.mult))

            weights_lo(0, N_A)
            dve.wait_ge(s_lo, N_A)
            pick(0, agu, agu_blk, s_ablk)
            diagonals(0)
            x2_copy(0)
            x2_lo(0)
            b_lo(0)
            body(0, True, False)
            with dve.Fori(1, NBLK - 1) as j:
                body(j, False, False)
            body(NBLK - 1, False, True)
            z3_mask(NBLK - 1)


_INS = ["x", "itok_B_1_198", "itok_B_0_7", "fside_8xS_0", "itok_B_0_6", "L0_cond_weights", "L1_cond_weights",
        "L2_cond_Wg", "L2_cond_Wu", "L2_cond_Wd", "L2_cond_Ag", "L2_cond_Bg", "L2_cond_Au", "L2_cond_Bu",
        "L2_cond_Ad", "L2_cond_Bd", "L3_cond_W", "L3_cond_A", "L3_cond_Bm", "L3_cond_scalings"]


def kernel(**inputs):
    import numpy as _np
    import concourse.bacc as _bacc
    from concourse.bass_utils import run_bass_kernel_spmd as _run

    nc = _bacc.Bacc("TRN2", target_bir_lowering=False, num_devices=1)
    arrays, args = {}, []
    for name in _INS:
        a = _np.ascontiguousarray(inputs[name])
        arrays[f"in_{name}"] = a
        args.append(nc.dram_tensor(f"in_{name}", a.shape, mybir.dt.from_np(a.dtype), kind="ExternalInput").ap())
    out = nc.dram_tensor("out_x", (B, C, T), mybir.dt.float32, kind="ExternalOutput").ap()
    build(nc, *args, out)
    return _run(nc, [arrays], core_ids=[0]).results[0]["out_x"]
```

```python
from contextlib import ExitStack

import concourse.bass as bass
from concourse import mybir

B, C, T = 128, 32, 256
NSEL, NAD, RANK, FF = 200, 8, 16, 1024
P = 128
NT = B * C
BLK = 512
NBLK = NT // BLK
GRP = BLK // P
BPG = P // C
BPB = BLK // C
KT = T // P
MF = FF // P
WS = 256.0
INV = 1.0 / WS
Q = 32
SLOTS = 2


def build(nc, x, i0, i1, bias, i3, w0, w1, wg, wu, wd, ag, bg, au, bu, ad, bd, w3, a3, bm, scal, out):
    f32, f16, i32, u32 = mybir.dt.float32, mybir.dt.float16, mybir.dt.int32, mybir.dt.uint32
    ALU, ACT, AX = mybir.AluOpType, mybir.ActivationFunctionType, mybir.AxisListType

    w0_rows = w0.rearrange("s c d -> (s c) d")
    x_rows = x.rearrange("b c t -> (b c) t")
    out_rows = out.rearrange("b c t -> (b c) t")
    wd_v = wd.rearrange("(p m) n -> p m n", m=MF)
    ad_v = ad.rearrange("n (p m) r -> p n (m r)", m=MF)

    with ExitStack() as ctx:
        def sb(name, shape, dt=f32):
            return ctx.enter_context(nc.sbuf_tensor(name, shape, dt))

        def sem(name):
            return ctx.enter_context(nc.semaphore(name))

        iota_p = sb("iota_p", [P, 1], i32)
        iota_q = sb("iota_q", [P, 1], i32)
        iota_r = sb("iota_r", [P, P], i32)
        pidx = sb("pidx", [P, 1])
        pmod = sb("pmod", [P, 1])
        ident = sb("ident", [P, P])
        eye32 = sb("eye32", [P, C])
        icol = sb("icol", [P, 3], i32)
        icolf = sb("icolf", [P, 4])
        vals = sb("vals", [P, 4, P], f16)
        own = sb("own", [P, NAD], f16)
        later = sb("later", [P, P], f16)
        one16 = sb("one16", [P, P], f16)
        tie = sb("tie", [P, NAD])
        left = sb("left", [P, NBLK, NAD])
        top = sb("top", [P, NBLK, 8])
        change = sb("change", [P, NBLK])
        is_most = sb("is_most", [P, NAD])
        others = sb("others", [P, NAD])
        prod = sb("prod", [P, NBLK, NAD])
        prod2 = sb("prod2", [P, NBLK, NAD])
        rank_all = sb("rank_all", [P, NAD])
        rank = sb("rank", [P, 1])
        mine = sb("mine", [P, NBLK])
        is_l, is_s = sb("is_l", [P, NBLK]), sb("is_s", [P, NBLK])
        turn = sb("turn", [P, NBLK])
        base_i = sb("base_i", [P, NBLK])
        as_l, as_s, turn_l, slot_l, slot_s = (sb(n, [P, NBLK]) for n in (
            "as_l", "as_s", "turn_l", "slot_l", "slot_s"))
        slots2 = sb("slots2", [P, 2, NBLK])
        slot_i = sb("slot_i", [P, 1], i32)
        edge_batches = sb("edge_batches", [1, 2, BPG], i32)
        last_p = sb("last_p", [P, NBLK])
        slot = sb("slot", [P, 1])
        deal = sb("deal", [P, P], f16)
        perm = sb("perm", [P, 2, B])
        rows = sb("rows", [P, 2, NT // P], u32)
        rows_blk = sb("rows_blk", [P, 2, GRP], u32)
        rows_out = sb("rows_out", [P, GRP], u32)
        prim = sb("prim", [P, 1])
        rp = sb("rp", [P, 1])
        ad_p, ad_s, ad_x = (sb(n, [P, NBLK]) for n in ("ad_p", "ad_s", "ad_x"))
        ids = sb("ids", [1, SLOTS, NBLK], i32)
        rows_b = sb("rows_b", [P, NBLK], u32)
        rows_b_blk = sb("rows_b_blk", [P, 1], u32)
        first_p = sb("first_p", [P, NBLK, BPB])
        quad = sb("quad", [P, 1])
        group_p = sb("group_p", [P, NBLK, GRP])
        group_s = sb("group_s", [P, NBLK, GRP])
        mask2 = sb("mask2", [P, B])
        rel = sb("rel", [P, B])
        ge0 = sb("ge0", [P, B])
        mask3 = sb("mask3", [P, B])
        mask3s = sb("mask3s", [P, B])
        scol = sb("scol", [P, 1])
        bias_tab = sb("bias_tab", [P, NAD, C])
        rest_p = sb("rest_p", [P, NBLK, BPB])

        wgu_raw = sb("wgu_raw", [P, 2, KT, FF])
        wd_raw = sb("wd_raw", [P, MF, T])
        agu_raw = sb("agu_raw", [P, 2, NAD, KT, RANK])
        ad_raw = sb("ad_raw", [P, NAD, MF, RANK])
        y = sb("y", [P, GRP, T])
        w3_raw, a3_raw = y[:, 0:KT, :], y[:, KT, :]
        bm_raw = y[:, KT + 1, :].rearrange("p (k n r) -> p k n r", k=KT, n=NAD)
        w3_f = sb("w3_f", [P, KT, T])
        ab3_f = sb("ab3_f", [P, 2, T])
        wgu = sb("wgu", [P, 2, 2, KT, MF, P], f16)
        wdd = sb("wdd", [P, 2, MF, T], f16)
        agu = sb("agu", [P, NAD, KT, 2, 2, RANK], f16)
        add = sb("add", [P, NAD, MF, 2, RANK], f16)
        w3t = sb("w3t", [P, 2, KT, T], f16)
        ab3 = sb("ab3", [P, 2, 2, T], f16)

        x0 = sb("x0", [P, GRP, T])
        agu_blk = sb("agu_blk", [P, KT, 4, SLOTS, RANK], f16)
        add_blk = sb("add_blk", [P, MF, 4, SLOTS, RANK], f16)
        bgu_got = sb("bgu_got", [P, 2, FF])
        bd_got = sb("bd_got", [P, T])
        bgu_blk = sb("bgu_blk", [P, 2, MF, P], f16)
        bd_blk = sb("bd_blk", [P, T], f16)
        got0 = sb("got0", [P, GRP, C])
        w1_tab = sb("w1_tab", [P, NAD, C])
        mat0, mat1 = sb("mat0", [P, GRP, C]), sb("mat1", [P, GRP, C])
        w1_p, w1_s = sb("w1_p", [P, GRP, C]), sb("w1_s", [P, GRP, C])
        diag0 = sb("diag0", [P, 2, GRP, P], f16)
        diag1 = sb("diag1", [P, 2, GRP, P], f16)
        x0s = sb("x0s", [P, 2, GRP, T], f16)
        x1s = sb("x1s", [P, 2, GRP, T], f16)
        bias_p, bias_s, bias_blk = (sb(n, [P, BPB, C]) for n in ("bias_p", "bias_s", "bias_blk"))
        x2f = sb("x2f", [P, KT, NT])
        x2s = sb("x2s", [P, 2, KT, BLK], f16)
        zf = sb("zf", [P, BLK])
        zg = sb("zg", [P, BLK], f16)
        zu = sb("zu", [P, BLK], f16)
        silu = sb("silu", [P, 2, BLK])
        table_warm = sb("table_warm", [P, 1])
        hf = sb("hf", [P, 2, BLK])
        hs = sb("hs", [P, 2, MF, BLK], f16)
        zdf = sb("zdf", [P, BLK])
        zds = sb("zds", [P, BLK], f16)
        x3f = sb("x3f", [P, KT, BLK])
        x3s = sb("x3s", [P, 2, KT, BLK], f16)
        z3f = sb("z3f", [P, BLK])
        z3s = sb("z3s", [P, 2, BLK], f16)

        bank = [ctx.enter_context(nc.psum_tensor(f"bank{i}", [P, BLK], f32)) for i in range(8)]
        gate_ps, up_ps = bank[0:2], bank[2:4]
        za_ps, zb_ps = bank[4], bank[5]
        pair_ps = bank[6:8]

        s_small, s_y = sem("small_loaded"), sem("y_stored")
        s_x0 = [sem(f"x0_half_{h}_loaded") for h in range(2)]
        s_w = {k: sem(f"{k}_loaded") for k in ("agu", "wgu0", "wgu1", "wd", "ad", "st3")}
        s_iota, s_rows, s_rowsblk, s_got, s_diag = (sem(n) for n in (
            "iota_done", "rows_done", "rows_blk_done", "rows_gathered", "diag_built"))
        s_zero, s_chain = sem("constants_written"), sem("vector_chain")
        s_icol = [sem(f"index_column_{n}_loaded") for n in range(3)]
        s_own, s_count, s_rank, s_deal, s_perm = (sem(n) for n in (
            "own_done", "counts_done", "ranks_done", "deal_done", "perm_done"))
        s_rowsb, s_bgot, s_bhi, s_blo, s_bdhi, s_bdlo, s_ablk, s_dblk, s_rowsout = (sem(n) for n in (
            "rows_b_copied", "b_gathered", "b_hi", "b_lo", "b_down_hi", "b_down_lo", "a_picked", "a_down_picked",
            "rows_out_copied"))
        s_w1, s_w1s = sem("w1_loaded"), sem("w1_masked")
        s_hi, s_lo, s_uplo = sem("weights_hi"), sem("a_weights_lo"), sem("gate_up_weights_lo")
        s_scaled, s_lo_pool = sem("weights_scaled"), sem("down_and_stage3_weights_lo")
        s_t3, s_t3f = sem("transposed"), sem("transposed_copied")
        s_vals, s_ident = sem("vals_done"), sem("identity_done")
        s_diag1 = sem("diag1_built")
        s_mat0, s_mat1, s_hi0, s_hi1 = sem("mat0_done"), sem("mat1_done"), sem("diag0_hi_done"), sem("diag1_hi_done")
        s_edge, s_x0sp, s_ylast = sem("edge_batches_done"), sem("x0_last_group_loaded"), sem("last_group_stored")
        s_masks = sem("masks_done")
        s_biases, s_bias = sem("bias_parts_done"), sem("bias_done")
        s_ready = sem("gather_may_start")
        pe_x1, pe_x2, pe_z, pe_gate, pe_up, pe_zd, pe_d, pe_z3, pe_y = (sem(n) for n in (
            "pe_x1", "pe_x2", "pe_z", "pe_gate", "pe_up", "pe_zd", "pe_down", "pe_z3", "pe_y"))
        x0hi_done, x0lo_done, x1hi_done, x1lo_done = (sem(n) for n in (
            "x0hi_done", "x0lo_done", "x1hi_done", "x1lo_done"))
        x2f_done, x2hi_done, x2lo_done = sem("x2f_done"), sem("x2hi_done"), sem("x2lo_done")
        zf_done, zhi_done, zlo_done = sem("zf_done"), sem("zhi_done"), sem("zlo_done")
        silu_done, hf_done, hhi_done, hlo_done = sem("silu_done"), sem("hf_done"), sem("hhi_done"), sem("hlo_done")
        zdf_done, zdhi_done, zdlo_done = sem("zdf_done"), sem("zdhi_done"), sem("zdlo_done")
        x3f_done, x3hi_done, x3lo_done = sem("x3f_done"), sem("x3hi_done"), sem("x3lo_done")
        z3f_done, z3hi_done, z3lo_done = sem("z3f_done"), sem("z3hi_done"), sem("z3lo_done")
        y_done = sem("y_done")

        def cols(ap):
            return ap.rearrange("p (c m) -> p m c", m=MF)

        SPLITS = [("agu", agu_raw[:, u].rearrange("p n k r -> p (n k) r"),
                   agu[:, :, :, u, 0, :].rearrange("p n k r -> p (n k) r"),
                   agu[:, :, :, u, 1, :].rearrange("p n k r -> p (n k) r")) for u in range(2)]
        N_A = len(SPLITS)
        SPLITS += [(f"wgu{k}", cols(wgu_raw[:, u, k, :]), wgu[:, 0, u, k], wgu[:, 1, u, k])
                   for k in range(KT) for u in range(2)]
        N_UP = len(SPLITS)
        SPLITS += [("ad", ad_raw[:].rearrange("p n m r -> p (n m) r"),
                    add[:, :, :, 0, :].rearrange("p n m r -> p (n m) r"),
                    add[:, :, :, 1, :].rearrange("p n m r -> p (n m) r")),
                   ("wd", wd_raw[:], wdd[:, 0], wdd[:, 1])]
        N_DOWN = len(SPLITS)
        W_LOADED = {"agu": 16 * 2 * KT, "wgu0": 32, "wgu1": 32, "ad": 16, "wd": 16}

        def half_block(h):
            return slice(h * BLK // 2, (h + 1) * BLK // 2)

        def adapters(eng, b):
            return [eng.value_load(ids[0:1, s, bass.ds(b, 1)], min_val=0, max_val=NAD - 1) for s in range(SLOTS)]

        def biases(eng, b, ad):
            for a, slots, dst in zip(ad, (first_p, rest_p), (bias_p, bias_s)):
                mask = slots[:, bass.ds(b, 1), :].rearrange("p i t -> p (i t)").unsqueeze(2)
                eng.tensor_tensor(dst[:], bias_tab[:, bass.ds(a, 1), :].to_broadcast([P, BPB, C]),
                                  mask.to_broadcast([P, BPB, C]), ALU.mult).then_inc(s_biases, 1)
            eng.wait_ge(s_biases, 2 * (b + 1))
            eng.tensor_tensor(bias_blk[:], bias_p[:], bias_s[:], ALU.add).then_inc(s_bias, 1)

        def after(eng, s, value):
            if not (isinstance(value, int) and value <= 0):
                eng.wait_ge(s, value)

        block = ctx.enter_context(nc.Block())

        @block.sync
        def _(sp):
            for n, v in ((1, i1), (0, i0), (2, i3)):
                sp.dma_start(icol[:, n:n + 1], v.rearrange("(b a) -> b a", a=1)).then_inc(s_icol[n], 16)
            sp.dma_start(bias_tab[:], bias.unsqueeze(0).to_broadcast([P, NAD, C])).then_inc(s_small, 16)
            sp.dma_start(scol[:], scal.rearrange("(n a) -> n a", a=1).unsqueeze(1).to_broadcast([NAD, RANK, 1])
                         ).then_inc(s_small, 16)
            for k in range(KT):
                for u, w in enumerate((wg, wu)):
                    sp.dma_start(wgu_raw[:, u, k, :], w[k * P:(k + 1) * P, :]).then_inc(s_w[f"wgu{k}"], 16)
            sp.dma_start(wd_raw[:], wd_v).then_inc(s_w["wd"], 16)
            def batch_number(n, q):
                return sp.value_load(edge_batches[0:1, n, q:q + 1], min_val=0, max_val=B - 1)

            sp.wait_ge(s_edge, 1)
            for q in range(BPG):
                sp.dma_start(x0[q * C:(q + 1) * C, GRP - 1, :],
                             x[bass.ds(batch_number(0, q), 1)].rearrange("o c t -> (o c) t")).then_inc(s_x0sp, 16)
            batches = [batch_number(1, q) for q in range(BPG)]
            sp.wait_ge(y_done, 2 * (NBLK - 1) + GRP)
            for q, batch in enumerate(batches):
                sp.dma_start(out[bass.ds(batch, 1)].rearrange("o c t -> (o c) t"), y[q * C:(q + 1) * C, GRP - 1, :]
                             ).then_inc(s_ylast, 16)
            sp.wait_ge(s_ylast, 16 * BPG)

        @block.gpsimd
        def _(pool):
            nc.gpsimd.iota(iota_p[:], pattern=[[0, 1]], base=0, channel_multiplier=1).then_inc(s_iota, 1)
            for q in range(BPG):
                pool.wait_ge(s_iota, q + 1)
                nc.gpsimd.iota(iota_q[q * C:(q + 1) * C, :], pattern=[[0, 1]], base=0,
                               channel_multiplier=1).then_inc(s_iota, 1)
            pool.wait_ge(s_iota, BPG + 1)
            nc.gpsimd.iota(iota_r[:], pattern=[[1, P]], base=0, channel_multiplier=0).then_inc(s_iota, 1)
            nc.gpsimd.memset(one16[:], 1.0).then_inc(s_zero, 1)
            for a in range(NAD):
                nc.gpsimd.memset(tie[:, a:a + 1], 2.0 ** -(4 + a)).then_inc(s_zero, 1)
            nc.gpsimd.memset(diag0[:], 0.0).then_inc(s_zero, 1)
            nc.gpsimd.memset(diag1[:], 0.0).then_inc(s_zero, 1)
            for n in range(3):
                pool.wait_ge(s_icol[n], 16)
            for n, src in ((0, icol[:, 0:1]), (1, iota_p[:]), (2, icol[:, 1:2]), (3, icol[:, 2:3])):
                nc.gpsimd.tensor_copy(icolf[:, n:n + 1], src).then_inc(s_vals, 1)
            pool.wait_ge(s_vals, 4)
            nc.gpsimd.tensor_copy(vals[:], icolf[:].unsqueeze(2).to_broadcast([P, 4, P])).then_inc(s_vals, 1)

            def gather(got, table, rows_of, done):
                nc.gpsimd.indirect_dma_start(out=got, out_offset=None, in_=table,
                                             in_offset=bass.IndirectOffsetOnAxis(ap=rows_of, axis=0)
                                             ).then_inc(done, 16)

            def gather_x(table_rows, groups=GRP):
                for g in range(GRP):
                    gather(got0[:, g, :], w0_rows, table_rows[:, 0, g:g + 1], s_got)
                for g in range(groups):
                    gather(x0[:, g, :], x_rows, table_rows[:, 1, g:g + 1], s_x0[g // 2])

            def gather_b(table_rows):
                for table, got in ((bg, bgu_got[:, 0, :]), (bu, bgu_got[:, 1, :]), (bd, bd_got[:])):
                    gather(got, table.rearrange("n r f -> (n r) f"), table_rows, s_bgot)

            def scatter_y(b, last_block=False):
                nc.gpsimd.tensor_copy(rows_out[:], rows[:, 1, bass.ds(b * GRP, GRP)]).then_inc(s_rowsout, 1)
                pool.wait_ge(s_rowsout, b + 1)
                if not last_block:
                    pool.wait_ge(y_done, 2 * b + 2)
                pool.sem_inc(s_ready, 1)
                for g in range(GRP - 1 if last_block else GRP):
                    if last_block:
                        pool.wait_ge(y_done, 2 * b + g + 1)
                    nc.gpsimd.indirect_dma_start(
                        out=out_rows, out_offset=bass.IndirectOffsetOnAxis(ap=rows_out[:, g:g + 1], axis=0),
                        in_=y[:, g, :], in_offset=None).then_inc(s_y, 16)

            def weights_lo():
                for n, (src, hi, low) in enumerate(((wd_raw[:], wdd[:, 0], wdd[:, 1]),
                                                    (ab3_f[:], ab3[:, 0], ab3[:, 1]),
                                                    (w3_f[:], w3t[:, 0], w3t[:, 1]))):
                    pool.wait_ge(s_hi, N_DOWN + n)
                    nc.gpsimd.tensor_scalar(src, src, WS, None, ALU.mult).then_inc(s_scaled, 1)
                    pool.wait_ge(s_scaled, n + 1)
                    nc.gpsimd.tensor_tensor(low, src, hi, ALU.subtract).then_inc(s_lo_pool, 1)

            def next_gathers(j, first=False):
                pool.wait_ge(s_mat0, j + 1)
                pool.wait_ge(x0lo_done, 2 * (j + 1))
                pool.sem_inc(s_ready, 1)
                nc.gpsimd.tensor_copy(rows_blk[:], rows[:, :, bass.ds((j + 1) * GRP, GRP)]).then_inc(s_rowsblk, 1)
                pool.wait_ge(s_rowsblk, j + 1)
                pool.sem_inc(s_ready, 1)
                gather_x(rows_blk)
                if first:
                    weights_lo()
                pool.wait_ge(s_blo, 2 * (j + 1))
                pool.wait_ge(s_bdlo, j + 1)
                pool.sem_inc(s_ready, 1)
                nc.gpsimd.tensor_copy(rows_b_blk[:], rows_b[:, bass.ds(j + 1, 1)]).then_inc(s_rowsb, 1)
                pool.wait_ge(s_rowsb, j + 1)
                pool.sem_inc(s_ready, 1)
                gather_b(rows_b_blk[:, 0:1])

            pool.wait_ge(s_rows, BPG)
            gather_x(rows, GRP - 1)
            pool.wait_ge(s_rows, BPG + 1)
            gather_b(rows_b[:, 0:1])
            pool.wait_ge(s_masks, 1)
            pool.wait_ge(s_small, 32)
            biases(pool, 0, adapters(pool, 0))
            next_gathers(0, True)
            with pool.Fori(1, NBLK - 1) as j:
                next_gathers(j)
                scatter_y(j - 1)
                pool.wait_ge(s_y, 16 * GRP * j)
                pool.sem_inc(s_ready, 1)
            scatter_y(NBLK - 2)
            pool.wait_ge(s_y, 16 * GRP * (NBLK - 1))
            scatter_y(NBLK - 1, True)
            pool.wait_ge(s_y, 16 * (GRP * NBLK - 1))

        @block.tensor
        def _(pe):
            def three(ps, whi, wlo, vhi, vlo, start, stop):
                nc.tensor.matmul(ps, whi, vhi, start=start, stop=False)
                nc.tensor.matmul(ps, wlo, vhi, start=False, stop=False)
                return nc.tensor.matmul(ps, whi, vlo, start=False, stop=stop)

            def keep_warm(n):
                for _ in range(n):
                    nc.tensor.matmul(gate_ps[0][:], one16[:], vals[:].rearrange("p n c -> p (n c)"),
                                     start=True, stop=True)

            def mix0(b, fill=0):
                pe.wait_ge(s_diag, 4 * (b + 1))
                for g in range(GRP):
                    if g == 2:
                        keep_warm(fill)
                    if g % 2 == 0:
                        pe.wait_ge(x0lo_done, 2 * b + g // 2 + 1)
                    last = three(pair_ps[g // 2][:, (g % 2) * T:(g % 2 + 1) * T], diag0[:, 0, g, :],
                                 diag0[:, 1, g, :], x0s[:, 0, g, :], x0s[:, 1, g, :], True, True)
                    if g % 2:
                        last.then_inc(pe_x1, 1)

            def mix1(b):
                pe.wait_ge(x1lo_done, 2 * (b + 1))
                pe.wait_ge(s_diag1, 4 * (b + 1))
                for k in range(KT):
                    cut = slice(k * P, (k + 1) * P)
                    for g in range(GRP):
                        last = three(pair_ps[k][:, g * P:(g + 1) * P], x1s[:, 0, g, cut], x1s[:, 1, g, cut],
                                     diag1[:, 0, g, :], diag1[:, 1, g, :], True, True)
                    last.then_inc(pe_x2, 1)

            def lora3(b, k):
                pe.wait_ge(x3lo_done, 2 * b + k + 1)
                cut = slice(k * P, (k + 1) * P)
                last = three(zb_ps[:], ab3[:, 0, 0, cut], ab3[:, 1, 0, cut], x3s[:, 0, k], x3s[:, 1, k],
                             k == 0, k == KT - 1)
                if k == KT - 1:
                    last.then_inc(pe_z3, 1)

            def main3(ps, g, k):
                cut = slice(g * P, (g + 1) * P)
                three(ps, x3s[:, 0, k, cut], x3s[:, 1, k, cut], w3t[:, 0, k], w3t[:, 1, k], k == 0, False)

            def back3(ps, g):
                cut = slice(g * P, (g + 1) * P)
                return three(ps, z3s[:, 0, cut], z3s[:, 1, cut], ab3[:, 0, 1], ab3[:, 1, 1], False, True)

            def out3(b):
                pe.wait_ge(z3lo_done, b + 1)
                for g in range(GRP):
                    ps = pair_ps[g // 2][:, (g % 2) * T:(g % 2 + 1) * T]
                    for k in range(KT):
                        main3(ps, g, k)
                    last = back3(ps, g)
                    if g % 2:
                        last.then_inc(pe_y, 1)

            def stage3_last(b):
                for k in range(KT):
                    lora3(b, k)
                    for g in range(GRP):
                        main3(bank[g][:, 0:T], g, k)
                for g in range(GRP):
                    if g % 2 == 0:
                        pe.wait_ge(z3lo_done, b + 1 + g // 2)
                    back3(bank[g][:, 0:T], g).then_inc(pe_y, 1)

            def body(j, first, last_block):
                pe.wait_ge(s_ablk, 2 * (j + 1))
                if not first:
                    pe.wait_ge(zdf_done, j)
                for k in range(KT):
                    pe.wait_ge(x2lo_done, 2 * j + k + 1)
                    for h in range(2):
                        last = nc.tensor.matmul(za_ps[:], agu_blk[:, k].rearrange("p q s r -> p (q s r)"),
                                                x2s[:, h, k], start=k + h == 0, stop=k + h == KT)
                last.then_inc(pe_z, 1)

                def dense(m):
                    if first:
                        pe.wait_ge(s_uplo, 4 if m < 2 else 8 if m < 4 else 12)
                    for ps, u, free in ((gate_ps[m % 2], 0, silu_done), (up_ps[m % 2], 1, hf_done)):
                        if not first or m >= 2:
                            pe.wait_ge(free, 8 * j + m - 1)
                        for k in range(KT):
                            three(ps[:], wgu[:, 0, u, k, m], wgu[:, 1, u, k, m], x2s[:, 0, k], x2s[:, 1, k],
                                  k == 0, False)

                def lora(m):
                    nc.tensor.matmul(gate_ps[m % 2][:], bgu_blk[:, 0, m], zg[:], start=False, stop=True
                                     ).then_inc(pe_gate, 1)
                    nc.tensor.matmul(up_ps[m % 2][:], bgu_blk[:, 1, m], zu[:], start=False, stop=True
                                     ).then_inc(pe_up, 1)

                for m in range(MF):
                    if m != 1:
                        dense(m)
                    if m == 0:
                        dense(1)
                        if not first:
                            for k in range(KT):
                                lora3(j - 1, k)
                        pe.wait_ge(zhi_done, 4 * (j + 1))
                        pe.wait_ge(zlo_done, 2 * (j + 1))
                        pe.wait_ge(s_blo, 2 * (j + 1))
                    lora(m)
                    if m == 1 and first:
                        pe.wait_ge(s_w["st3"], 16 * 4)
                        pe.wait_ge(s_ident, 1)
                        for k in range(KT):
                            nc.tensor.transpose(zb_ps[:, k * P:(k + 1) * P], a3_raw[:, k * P:(k + 1) * P], ident[:])
                            last = nc.tensor.transpose(zb_ps[:, T + k * P:T + (k + 1) * P],
                                                       bm_raw[:, k].rearrange("p n r -> p (n r)"), ident[:])
                        last.then_inc(s_t3, 1)
                        for k in range(KT):
                            for o in range(KT):
                                last = nc.tensor.transpose(pair_ps[0][:, k * T + o * P:k * T + (o + 1) * P],
                                                           w3_raw[:, o, k * P:(k + 1) * P], ident[:])
                        last.then_inc(s_t3, 1)
                    if m == 3 and not first:
                        out3(j - 1)
                    if m == 5 and not last_block:
                        if first:
                            pe.wait_ge(s_t3f, 3)
                        else:
                            pe.wait_ge(y_done, 2 * j)
                        mix0(j + 1)
                if not last_block:
                    mix1(j + 1)
                if first:
                    pe.wait_ge(s_lo_pool, 1)
                pe.wait_ge(s_dblk, 4 * (j + 1))
                for m in range(MF):
                    pe.wait_ge(hlo_done, 8 * j + m + 1)
                    for h in range(2):
                        last = nc.tensor.matmul(za_ps[:], add_blk[:, m].rearrange("p q s r -> p (q s r)"),
                                                hs[:, h, m], start=m + h == 0, stop=m + h == MF)
                last.then_inc(pe_zd, 1)
                if last_block:
                    pe.wait_ge(y_done, 2 * j)
                else:
                    pe.wait_ge(x2f_done, 2 * (j + 2))
                for c in range(KT):
                    cut = slice(c * P, (c + 1) * P)
                    for m in range(MF):
                        three(pair_ps[c][:], wdd[:, 0, m, cut], wdd[:, 1, m, cut], hs[:, 0, m], hs[:, 1, m],
                              m == 0, False)
                    if c == 0:
                        pe.wait_ge(zdlo_done, j + 1)
                        pe.wait_ge(s_bdlo, j + 1)
                    nc.tensor.matmul(pair_ps[c][:], bd_blk[:, cut], zds[:], start=False, stop=True
                                     ).then_inc(pe_d, 1)

            pe.wait_ge(s_zero, 1)
            pe.wait_ge(s_own, 1)
            nc.tensor.matmul(zb_ps[:, 0:NAD], one16[:], own[:], start=True, stop=True).then_inc(s_count, 1)
            pe.wait_ge(s_own, 2)
            nc.tensor.matmul(za_ps[:, 0:NAD], later[:], own[:], start=True, stop=True).then_inc(s_rank, 1)
            pe.wait_ge(s_deal, 1)
            pe.wait_ge(s_vals, 5)
            for n in range(4):
                last = nc.tensor.matmul(zb_ps[:, n * P:(n + 1) * P], vals[:, n, :], deal[:], start=True, stop=True)
            last.then_inc(s_perm, 1)
            pe.wait_ge(s_lo, N_A)
            keep_warm(14)
            mix0(0, 2)
            keep_warm(5)
            mix1(0)
            keep_warm(7)
            body(0, True, False)
            pe.wait_ge(s_lo_pool, 3)
            with pe.Fori(1, NBLK - 1) as j:
                body(j, False, False)
            body(NBLK - 1, False, True)
            stage3_last(NBLK - 1)

        @block.scalar
        def _(act):
            def half(dst, src, scale=1.0):
                return nc.scalar.activation(dst, src, ACT.Copy, scale=scale)

            for u, a in enumerate((ag, au)):
                for k in range(KT):
                    act.dma_start(agu_raw[:, u, :, k, :], a[:, k * P:(k + 1) * P, :].rearrange("n p r -> p n r")
                                  ).then_inc(s_w["agu"], 16)
            act.dma_start(ad_raw[:].rearrange("p n m r -> p n (m r)"), ad_v).then_inc(s_w["ad"], 16)
            for q in range(BPG):
                act.dma_start(w1_tab[q * C:(q + 1) * C], w1.rearrange("n c d -> c n d")).then_inc(s_w1, 16)
            act.dma_start(w3_raw, w3.rearrange("(o p) i -> p o i", p=P)).then_inc(s_w["st3"], 16)
            act.dma_start(a3_raw, a3.rearrange("n r i -> (n r) i")).then_inc(s_w["st3"], 16)
            for k in range(KT):
                act.dma_start(bm_raw[:, k], bm[:, k * P:(k + 1) * P, :].rearrange("n p r -> p n r")
                              ).then_inc(s_w["st3"], 16)

            def x0_hi(b, first=False):
                for h in range(2):
                    act.wait_ge(s_x0[h], 32 * (b + 1) - 16 * h)
                    if first and h == 1:
                        act.wait_ge(s_x0sp, 16 * BPG)
                    half(x0s[:, 0, 2 * h:2 * h + 2, :], x0[:, 2 * h:2 * h + 2, :]).then_inc(x0hi_done, 1)

            def x1_hi(b):
                for h in range(2):
                    act.wait_ge(pe_x1, 2 * b + h + 1)
                    half(x1s[:, 0, 2 * h:2 * h + 2, :].rearrange("p g t -> p (g t)"), pair_ps[h][:], INV
                         ).then_inc(x1hi_done, 1)

            def x2_hi(b):
                for k in range(KT):
                    act.wait_ge(x2f_done, 2 * b + k + 1)
                    half(x2s[:, 0, k], x2f[:, k, bass.ds(b * BLK, BLK)]
                         ).then_inc(x2hi_done, 1)

            def y_copy(b):
                for h in range(2):
                    act.wait_ge(pe_y, 2 * b + h + 1)
                    half(y[:, 2 * h:2 * h + 2, :].rearrange("p g t -> p (g t)"), pair_ps[h][:], INV
                         ).then_inc(y_done, 1)

            def y_copy_last(b):
                for g in range(GRP):
                    act.wait_ge(pe_y, 2 * b + g + 1)
                    half(y[:, g, :], bank[g][:, 0:T], INV).then_inc(y_done, 1)

            def z3_hi(b):
                act.wait_ge(z3f_done, b + 1)
                half(z3s[:, 0], z3f[:]).then_inc(z3hi_done, 1)

            def z3_hi_last(b):
                for h in range(2):
                    act.wait_ge(z3f_done, b + 1 + h)
                    half(z3s[:, 0, half_block(h)], z3f[:, half_block(h)]).then_inc(z3hi_done, 1)

            def weights_hi(a, b):
                for name, src, hi, _ in SPLITS[a:b]:
                    act.wait_ge(s_w[name], W_LOADED[name])
                    half(hi, src, WS).then_inc(s_hi, 1)

            def b_hi(b):
                act.wait_ge(s_bgot, 48 * (b + 1))
                for u in range(2):
                    half(bgu_blk[:, u], cols(bgu_got[:, u, :]), WS).then_inc(s_bhi, 1)

            def h_hi(j, m):
                act.wait_ge(hf_done, 8 * j + m + 1)
                half(hs[:, 0, m], hf[:, m % 2]).then_inc(hhi_done, 1)

            def body(j, first, last_block):
                act.wait_ge(zf_done, j + 1)
                half(zg[0:2 * Q], zf[0:2 * Q]).then_inc(zhi_done, 1)
                half(zu[2 * Q:4 * Q], zf[2 * Q:4 * Q]).then_inc(zhi_done, 1)
                half(zg[3 * Q:4 * Q], zf[0:Q]).then_inc(zhi_done, 1)
                half(zu[Q:2 * Q], zf[2 * Q:3 * Q]).then_inc(zhi_done, 1)
                for m in range(MF):
                    act.wait_ge(pe_gate, 8 * j + m + 1)
                    nc.scalar.activation(silu[:, m % 2], gate_ps[m % 2][:], ACT.Silu, scale=INV
                                         ).then_inc(silu_done, 1)
                    if m:
                        h_hi(j, m - 1)
                    if m == 0 and not first:
                        z3_hi(j - 1)
                    if m == 4 and first:
                        act.wait_ge(s_t3f, 1)
                        half(ab3[:, 0], ab3_f[:], WS).then_inc(s_hi, 1)
                        act.wait_ge(s_t3f, 3)
                        half(w3t[:, 0], w3_f[:], WS).then_inc(s_hi, 1)
                    if m == 4 and not first:
                        y_copy(j - 1)
                    if m == 5:
                        half(bd_blk[:], bd_got[:], WS).then_inc(s_bdhi, 1)
                    if m == 2 and not last_block:
                        x0_hi(j + 1)
                    if m == 5 and not last_block:
                        x1_hi(j + 1)
                h_hi(j, MF - 1)
                if not last_block:
                    x2_hi(j + 1)
                act.wait_ge(zdf_done, j + 1)
                half(zds[:], zdf[:]).then_inc(zdhi_done, 1)
                if not last_block:
                    b_hi(j + 1)
                for c in range(KT):
                    act.wait_ge(x3f_done, 2 * j + c + 1)
                    half(x3s[:, 0, c], x3f[:, c]).then_inc(x3hi_done, 1)
                if not first:
                    act.wait_ge(s_y, 16 * GRP * j)

            act.wait_ge(s_zero, 1)
            nc.scalar.activation(table_warm[:], one16[:, 0:1], ACT.Silu)
            weights_hi(0, N_DOWN)
            x0_hi(0, True)
            x1_hi(0)
            x2_hi(0)
            b_hi(0)
            body(0, True, False)
            with act.Fori(1, NBLK - 1) as j:
                body(j, False, False)
            body(NBLK - 1, False, True)
            z3_hi_last(NBLK - 1)
            y_copy_last(NBLK - 1)

        @block.vector
        def _(dve):
            chain = [0]

            def link(ins):
                chain[0] += 1
                ins.then_inc(s_chain, 1)
                dve.wait_ge(s_chain, chain[0])

            def lo(dst, src, hi, scale=1.0):
                if scale == 1.0:
                    return nc.vector.tensor_tensor(dst, src, hi, ALU.subtract)
                return nc.vector.scalar_tensor_tensor(dst, src, scale, hi, ALU.mult, ALU.subtract)

            def by_batch(ap, b):
                return ap[:, bass.ds(b * BPB, BPB)].unsqueeze(2).to_broadcast([P, BPB, C])

            def tokens(ap):
                return ap.rearrange("p (b c) -> p b c", c=C)

            def diagonal(mat, diag, his, done, b):
                for q in range(BPG):
                    part = slice(q * C, (q + 1) * C)
                    nc.vector.tensor_copy(diag[part, 0, :, part], mat[part]).then_inc(his, 1)
                for q in range(BPG):
                    part = slice(q * C, (q + 1) * C)
                    dve.wait_ge(his, 4 * b + q + 1)
                    lo(diag[part, 1, :, part], mat[part], diag[part, 0, :, part]).then_inc(done, 1)

            def diagonals0(b):
                dve.wait_ge(s_got, 16 * GRP * (b + 1))
                after(dve, s_diag, 4 * b)
                nc.vector.scalar_tensor_tensor(mat0[:], got0[:], WS, eye32[:].unsqueeze(1).to_broadcast([P, GRP, C]),
                                               ALU.mult, ALU.add).then_inc(s_mat0, 1)
                dve.wait_ge(s_mat0, b + 1)
                diagonal(mat0, diag0, s_hi0, s_diag, b)

            def picked1(b, ad):
                after(dve, s_diag1, 4 * b)
                for a, mask, dst in zip(ad, (group_p, group_s), (w1_p, w1_s)):
                    nc.vector.tensor_tensor(dst[:], w1_tab[:, bass.ds(a, 1), :].to_broadcast([P, GRP, C]),
                                            mask[:, bass.ds(b, 1), :].rearrange("p i g -> p (i g)").unsqueeze(2)
                                            .to_broadcast([P, GRP, C]), ALU.mult).then_inc(s_w1s, 1)
                dve.wait_ge(s_w1s, 2 * (b + 1))
                nc.vector.tensor_tensor(mat1[:], w1_p[:], w1_s[:], ALU.add).then_inc(s_mat1, 1)

            def diagonals1(b):
                dve.wait_ge(s_mat1, b + 1)
                diagonal(mat1, diag1, s_hi1, s_diag1, b)

            def x0_lo(b, halves=range(2)):
                for h in halves:
                    dve.wait_ge(x0hi_done, 2 * b + h + 1)
                    cut = slice(2 * h, 2 * h + 2)
                    lo(x0s[:, 1, cut, :], x0[:, cut, :], x0s[:, 0, cut, :]).then_inc(x0lo_done, 1)

            def x1_lo(b, halves=range(2)):
                for h in halves:
                    dve.wait_ge(x1hi_done, 2 * b + h + 1)
                    his, los = (x1s[:, n, 2 * h:2 * h + 2, :].rearrange("p g t -> p (g t)") for n in range(2))
                    lo(los, pair_ps[h][:], his, INV).then_inc(x1lo_done, 1)

            def x2_copy(b):
                dve.wait_ge(s_bias, b + 1)
                for k in range(KT):
                    dve.wait_ge(pe_x2, 2 * b + k + 1)
                    dst = x2f[:, k, bass.ds(b * BLK, BLK)]
                    nc.vector.scalar_tensor_tensor(dst, pair_ps[k][:], INV, bias_blk[:].rearrange("p b c -> p (b c)"),
                                                   ALU.mult, ALU.add).then_inc(x2f_done, 1)

            def x2_lo(b):
                for k in range(KT):
                    dve.wait_ge(x2hi_done, 2 * b + k + 1)
                    src = x2f[:, k, bass.ds(b * BLK, BLK)]
                    lo(x2s[:, 1, k], src, x2s[:, 0, k]).then_inc(x2lo_done, 1)

            def z3_mask(b):
                dve.wait_ge(pe_z3, b + 1)
                nc.vector.tensor_tensor(tokens(z3f[:]), tokens(zb_ps[:]), by_batch(mask3s, b), ALU.mult
                                        ).then_inc(z3f_done, 1)
                dve.wait_ge(z3hi_done, b + 1)
                lo(z3s[:, 1], z3f[:], z3s[:, 0]).then_inc(z3lo_done, 1)
                dve.wait_ge(z3lo_done, b + 1)

            def weights_lo(a, b):
                for n, (_, src, hi, low) in enumerate(SPLITS[a:b], a):
                    dve.wait_ge(s_hi, n + 1)
                    lo(low, src, hi, WS).then_inc(s_lo, 1)

            def z3_last(b):
                dve.wait_ge(pe_z3, b + 1)
                for h in range(2):
                    cut = half_block(h)
                    nc.vector.tensor_tensor(tokens(z3f[:, cut]), tokens(zb_ps[:, cut]),
                                            mask3s[:, bass.ds(b * BPB + h * BPB // 2, BPB // 2)].unsqueeze(2)
                                            .to_broadcast([P, BPB // 2, C]), ALU.mult).then_inc(z3f_done, 1)
                for h in range(2):
                    cut = half_block(h)
                    dve.wait_ge(z3hi_done, b + 1 + h)
                    lo(z3s[:, 1, cut], z3f[:, cut], z3s[:, 0, cut]).then_inc(z3lo_done, 1)

            def up_lo(m, n):
                for i, (_, src, hi, low) in enumerate(SPLITS[N_A:N_UP], N_A):
                    dve.wait_ge(s_hi, i + 1)
                    lo(low[:, m:n], src[:, m:n], hi[:, m:n], WS).then_inc(s_uplo, 1)

            def b_lo(b):
                for u, q in ((0, 3), (1, 1)):
                    part = slice(q * Q, (q + 1) * Q)
                    dve.wait_ge(s_bhi, 2 * b + u + 1)
                    lo(bgu_blk[part, u], cols(bgu_got[part, u, :]), bgu_blk[part, u], WS).then_inc(s_blo, 1)

            def pick(ad, table, blk, done):
                for s, a in enumerate(ad):
                    src = table[:, bass.ds(a, 1)]
                    if table is agu:
                        nc.vector.tensor_copy(blk[:, :, :, s, :].rearrange("p k q r -> p (k q) r"),
                                              src.rearrange("p n k u h r -> p (n k u h) r")).then_inc(done, 1)
                    else:
                        src = src.rearrange("p n m h r -> p (n m) h r")
                        nc.vector.tensor_copy(blk[:, :, 0:2, s, :], src).then_inc(done, 1)
                        nc.vector.tensor_copy(blk[:, :, 2:4, s, :], src[:, :, 0:1, :].to_broadcast([P, MF, 2, RANK])
                                              ).then_inc(done, 1)

            def h_lo(j, m):
                dve.wait_ge(hhi_done, 8 * j + m + 1)
                lo(hs[:, 1, m], hf[:, m % 2], hs[:, 0, m]).then_inc(hlo_done, 1)

            def body(j, first, last_block, ad0=None):
                dve.wait_ge(pe_z, j + 1)
                after(dve, zlo_done, 2 * j)
                nc.vector.tensor_tensor(tokens(zf[:]), tokens(za_ps[:]), by_batch(mask2, j), ALU.mult
                                        ).then_inc(zf_done, 1)
                if first:
                    b_lo(0)
                dve.wait_ge(zhi_done, 4 * (j + 1))
                lo(zg[2 * Q:3 * Q], zf[0:Q], zg[0:Q]).then_inc(zlo_done, 1)
                lo(zu[0:Q], zf[2 * Q:3 * Q], zu[2 * Q:3 * Q]).then_inc(zlo_done, 1)
                for m in range(MF):
                    dve.wait_ge(silu_done, 8 * j + m + 1)
                    dve.wait_ge(pe_up, 8 * j + m + 1)
                    if not first or m >= 2:
                        dve.wait_ge(hlo_done, 8 * j + m - 1)
                    nc.vector.scalar_tensor_tensor(hf[:, m % 2], up_ps[m % 2][:], INV, silu[:, m % 2],
                                                   ALU.mult, ALU.mult).then_inc(hf_done, 1)
                    if m:
                        h_lo(j, m - 1)
                    if m == 0 and not first:
                        z3_mask(j - 1)
                    if m == 0 and first:
                        up_lo(4, MF)
                    if m == 1 and first:
                        weights_lo(N_UP, N_UP + 1)
                    if m == 2 and not last_block:
                        diagonals0(j + 1)
                    if m == 3 and not last_block:
                        x0_lo(j + 1)
                    if m == 4 and not last_block:
                        ad = adapters(dve, j + 1)
                        picked1(j + 1, ad)
                        diagonals1(j + 1)
                    if m == 5 and not last_block:
                        x1_lo(j + 1)
                    if m == 5 and first:
                        dve.wait_ge(s_lo, N_A + 1)
                        pick(ad0, add, add_blk, s_dblk)
                    if m == 6:
                        dve.wait_ge(s_bdhi, j + 1)
                        lo(bd_blk[3 * Q:], bd_got[3 * Q:], bd_blk[3 * Q:], WS).then_inc(s_bdlo, 1)
                    if m == 6 and not last_block:
                        biases(dve, j + 1, ad)
                    if m == 3 and first:
                        dve.wait_ge(s_t3, 1)
                        nc.vector.tensor_copy(ab3_f[:].rearrange("p a t -> p (a t)"), zb_ps[:]).then_inc(s_t3f, 1)
                        dve.wait_ge(s_t3, 2)
                        for k in range(KT):
                            other = slice((1 - k) * P, (2 - k) * P)
                            link(nc.vector.tensor_copy(w3_f[:, k, other], pair_ps[0][:, k * T + (1 - k) * P:
                                                                                     k * T + (2 - k) * P]))
                            nc.vector.tensor_tensor(w3_f[:, k, k * P:(k + 1) * P],
                                                    pair_ps[0][:, k * T + k * P:k * T + (k + 1) * P],
                                                    ident[:], ALU.add).then_inc(s_t3f, 1)
                h_lo(j, MF - 1)
                if not last_block:
                    x2_copy(j + 1)
                    x2_lo(j + 1)
                if first:
                    link(tsc(rel[:], perm[:, 1, :], -float(RANK), pidx[:, 0:1], ALU.mult, ALU.add))
                    link(tsc(ge0[:], rel[:], 0.0, INV, ALU.is_ge, ALU.mult))
                    link(nc.vector.scalar_tensor_tensor(mask3[:], rel[:], float(RANK), ge0[:],
                                                        ALU.is_lt, ALU.mult))
                    link(tsc(mask3s[:], mask3[:], scol[:, 0:1], None, ALU.mult))
                dve.wait_ge(pe_zd, j + 1)
                after(dve, zdlo_done, j)
                nc.vector.tensor_tensor(tokens(zdf[:]), tokens(za_ps[:]), by_batch(mask2, j), ALU.mult
                                        ).then_inc(zdf_done, 1)
                dve.wait_ge(zdhi_done, j + 1)
                lo(zds[2 * Q:3 * Q], zdf[2 * Q:3 * Q], zds[2 * Q:3 * Q]).then_inc(zdlo_done, 1)
                if not last_block:
                    pick(ad, agu, agu_blk, s_ablk)
                    pick(ad, add, add_blk, s_dblk)
                    b_lo(j + 1)
                for c in range(KT):
                    dve.wait_ge(pe_d, 2 * j + c + 1)
                    after(dve, x3lo_done, 2 * j)
                    res = x2f[:, c, bass.ds(j * BLK, BLK)]
                    nc.vector.scalar_tensor_tensor(x3f[:, c], pair_ps[c][:], INV, res, ALU.mult, ALU.add
                                                   ).then_inc(x3f_done, 1)
                    dve.wait_ge(x3hi_done, 2 * j + c + 1)
                    lo(x3s[:, 1, c], x3f[:, c], x3s[:, 0, c]).then_inc(x3lo_done, 1)

            def tsc(out, src, a, b, op0, op1=None):
                return nc.vector.tensor_scalar(out, src, a, b, op0) if op1 is None else \
                    nc.vector.tensor_scalar(out, src, a, b, op0, op1)

            def over_blocks(ap):
                return ap.unsqueeze(1).to_broadcast([P, NBLK, NAD])

            def over_adapters(ap):
                return ap.unsqueeze(2).to_broadcast([P, NBLK, NAD])

            dve.wait_ge(s_iota, BPG + 2)
            nc.vector.tensor_copy(pmod[:], iota_q[:])
            link(nc.vector.tensor_copy(pidx[:], iota_p[:]))
            dve.wait_ge(s_icol[1], 16)
            tsc(own[:], iota_r[:, 0:NAD], icol[:, 1:2], None, ALU.is_equal).then_inc(s_own, 1)
            tsc(later[:], iota_r[:], pidx[:, 0:1], None, ALU.is_gt).then_inc(s_own, 1)
            tsc(ident[:], iota_r[:], pidx[:, 0:1], None, ALU.is_equal).then_inc(s_ident, 1)
            tsc(quad[:], pidx[:], pmod[:, 0:1], 1.0 / C, ALU.subtract, ALU.mult)
            tsc(base_i[:], iota_r[:, 0:NBLK], float(BPB), None, ALU.mult)
            dve.wait_ge(s_zero, 1 + NAD)
            dve.wait_ge(s_count, 1)
            link(nc.vector.tensor_tensor(left[:, 0, :], zb_ps[:, 0:NAD], tie[:], ALU.add))
            for i in range(NBLK):
                now = left[:, i, :]
                link(nc.vector.max(top[:, i, :], now))
                if i < NBLK - 1:
                    most, fewest = top[:, i, 0:1], top[:, i, 7 - i:8 - i]
                    tsc(change[:, i:i + 1], fewest, -float(BPB), None, ALU.add)
                    tsc(is_most[:], now, most, None, ALU.is_equal)
                    link(nc.vector.scalar_tensor_tensor(others[:], now, fewest, now, ALU.is_gt, ALU.mult))
                    link(nc.vector.scalar_tensor_tensor(left[:, i + 1, :], is_most[:], change[:, i:i + 1], others[:],
                                                        ALU.mult, ALU.add))
            tops = top[:].rearrange("p i a -> p (i a)")
            most, fewest = tops[:, 0:NBLK * 8:8], tops[:, 7:7 * NBLK + 1:7]
            dve.wait_ge(s_rank, 1)
            nc.vector.tensor_tensor(rank_all[:], za_ps[:, 0:NAD], own[:], ALU.mult)
            link(nc.vector.tensor_tensor(prod[:], left[:], over_blocks(own[:]), ALU.mult))
            nc.vector.reduce_sum(rank[:], rank_all[:], axis=AX.X)
            link(nc.vector.reduce_sum(mine[:], prod[:], axis=AX.X))
            tsc(turn[:], mine[:], mine[:, 0:1], rank[:, 0:1], ALU.subtract, ALU.add)
            nc.vector.tensor_tensor(is_l[:], mine[:], most, ALU.is_equal)
            link(nc.vector.tensor_tensor(is_s[:], mine[:], fewest, ALU.is_equal))
            nc.vector.tensor_tensor(turn_l[:], turn[:], fewest, ALU.add)
            nc.vector.scalar_tensor_tensor(as_s[:], turn[:], 0.0, is_s[:], ALU.is_ge, ALU.mult)
            nc.vector.scalar_tensor_tensor(as_l[:], turn[:], 0.0, is_l[:], ALU.is_ge, ALU.mult)
            link(nc.vector.tensor_tensor(slot_s[:], turn[:], base_i[:], ALU.add))
            nc.vector.tensor_tensor(slots2[:, 0, :], as_s[:], slot_s[:], ALU.mult)
            nc.vector.tensor_tensor(slot_l[:], turn_l[:], base_i[:], ALU.add)
            link(nc.vector.scalar_tensor_tensor(is_l[:], turn_l[:], float(BPB), as_l[:], ALU.is_lt, ALU.mult))
            link(nc.vector.tensor_tensor(slots2[:, 1, :], is_l[:], slot_l[:], ALU.mult))
            link(nc.vector.reduce_sum(slot[:], slots2[:].rearrange("p s i -> p (s i)"), axis=AX.X))
            link(nc.vector.tensor_copy(slot_i[:], slot[:]))
            link(nc.vector.tensor_copy(slot[:], slot_i[:]))
            tsc(deal[:], iota_r[:], slot[:, 0:1], None, ALU.is_equal).then_inc(s_deal, 1)
            nc.vector.tensor_tensor(prod[:], left[:], over_adapters(fewest), ALU.is_equal)
            link(nc.vector.tensor_tensor(prod2[:], left[:], over_adapters(most), ALU.is_equal))
            nc.vector.tensor_tensor(prod[:], prod[:], over_blocks(iota_r[:, 0:NAD]), ALU.mult)
            link(nc.vector.tensor_tensor(prod2[:], prod2[:], over_blocks(iota_r[:, 0:NAD]), ALU.mult))
            dve.wait_ge(s_perm, 1)
            groups = zb_ps[0:1, P:2 * P].rearrange("p (g b) -> p g b", b=BPG)
            nc.vector.tensor_copy(edge_batches[:], groups[:, GRP - 1::NT // P - GRP, :]).then_inc(s_edge, 1)
            for q in range(BPG):
                part = slice(q * C, (q + 1) * C)
                tsc(rows[part], zb_ps[part, 0:2 * P].rearrange("p (n g b) -> p n b g", n=2, b=BPG)[:, :, q, :],
                    float(C), pmod[part, 0:1], ALU.mult, ALU.add).then_inc(s_rows, 1)
            nc.vector.tensor_copy(perm[:].rearrange("p n b -> p (n b)"), zb_ps[:, 2 * P:4 * P])
            tsc(eye32[:], iota_r[:, 0:C], pmod[:, 0:1], WS, ALU.is_equal, ALU.mult)
            tsc(prim[:], pmod[:], float(RANK), None, ALU.is_lt)
            nc.vector.reduce_sum(ad_p[:], prod[:], axis=AX.X)
            link(nc.vector.reduce_sum(ad_s[:], prod2[:], axis=AX.X))
            tsc(rp[:], prim[:], float(RANK), pmod[:, 0:1], ALU.mult, ALU.add)
            nc.vector.tensor_copy(ids[0:1, 0, :], ad_p[0:1, :])
            nc.vector.tensor_copy(ids[0:1, 1, :], ad_s[0:1, :])
            link(nc.vector.tensor_tensor(ad_x[:], ad_p[:], ad_s[:], ALU.subtract))
            link(nc.vector.scalar_tensor_tensor(ad_x[:], ad_x[:], prim[:, 0:1], ad_s[:], ALU.mult, ALU.add))
            link(tsc(ad_x[:], ad_x[:], float(RANK), -float(RANK), ALU.mult, ALU.add))
            tsc(rows_b[:], ad_x[:], rp[:, 0:1], None, ALU.add).then_inc(s_rows, 1)
            link(tsc(last_p[:], fewest, -0.5, None, ALU.add))
            link(nc.vector.tensor_tensor(first_p[:], iota_r[:, 0:BPB].unsqueeze(1).to_broadcast([P, NBLK, BPB]),
                                         last_p[:].unsqueeze(2).to_broadcast([P, NBLK, BPB]), ALU.is_lt))
            tsc(rest_p[:], first_p[:], -1.0, 1.0, ALU.mult, ALU.add).then_inc(s_masks, 1)
            tsc(mask2[:], first_p[:].rearrange("p i t -> p (i t)"), prim[:, 0:1], INV, ALU.is_equal, ALU.mult)
            link(nc.vector.scalar_tensor_tensor(
                group_p[:], iota_r[:, 0:BPB:BPG].unsqueeze(1).to_broadcast([P, NBLK, GRP]), quad[:, 0:1],
                last_p[:].unsqueeze(2).to_broadcast([P, NBLK, GRP]), ALU.add, ALU.is_lt))
            link(tsc(group_s[:], group_p[:], -1.0, 1.0, ALU.mult, ALU.add))
            weights_lo(0, N_A)
            ad = adapters(dve, 0)
            dve.wait_ge(s_lo, N_A)
            pick(ad, agu, agu_blk, s_ablk)
            dve.wait_ge(s_w1, 16 * BPG)
            link(nc.vector.scalar_tensor_tensor(w1_tab[:], w1_tab[:], WS, eye32[:].unsqueeze(1).to_broadcast(
                [P, NAD, C]), ALU.mult, ALU.add))
            dve.wait_ge(s_small, 32)
            picked1(0, ad)
            dve.wait_ge(s_zero, 3 + NAD)
            diagonals0(0)
            diagonals1(0)
            x0_lo(0, [0])
            x0_lo(0, [1])
            up_lo(0, 2)
            x1_lo(0, [0])
            x1_lo(0, [1])
            x2_copy(0)
            x2_lo(0)
            up_lo(2, 4)
            body(0, True, False, ad)
            with dve.Fori(1, NBLK - 1) as j:
                body(j, False, False)
            body(NBLK - 1, False, True)
            z3_last(NBLK - 1)


_INS = ["x", "itok_B_1_198", "itok_B_0_7", "fside_8xS_0", "itok_B_0_6", "L0_cond_weights", "L1_cond_weights",
        "L2_cond_Wg", "L2_cond_Wu", "L2_cond_Wd", "L2_cond_Ag", "L2_cond_Bg", "L2_cond_Au", "L2_cond_Bu",
        "L2_cond_Ad", "L2_cond_Bd", "L3_cond_W", "L3_cond_A", "L3_cond_Bm", "L3_cond_scalings"]


def kernel(**inputs):
    import numpy as _np
    import concourse.bacc as _bacc
    from concourse.bass_utils import run_bass_kernel_spmd as _run

    nc = _bacc.Bacc("TRN2", target_bir_lowering=False, num_devices=1)
    arrays, args = {}, []
    for name in _INS:
        a = _np.ascontiguousarray(inputs[name])
        arrays[f"in_{name}"] = a
        args.append(nc.dram_tensor(f"in_{name}", a.shape, mybir.dt.from_np(a.dtype), kind="ExternalInput").ap())
    out = nc.dram_tensor("out_x", (B, C, T), mybir.dt.float32, kind="ExternalOutput").ap()
    build(nc, *args, out)
    return _run(nc, [arrays], core_ids=[0]).results[0]["out_x"]
```
